# Optimizing a Trainium2 kernel written in Bass

```python
import numpy as np
import jax
import jax.numpy as jnp

def _softmax(x, axis=-1):
    return jax.nn.softmax(x, axis=axis)

def _gelu(x):
    return jax.nn.gelu(x, approximate=True)

def _silu(x):
    return jax.nn.silu(x)

def _sigmoid(x):
    return jax.nn.sigmoid(x)

def _layernorm(x, axis=-1, eps=1e-05):
    m = jnp.mean(x, axis=axis, keepdims=True)
    v = jnp.var(x, axis=axis, keepdims=True)
    return (x - m) / jnp.sqrt(v + eps)

def _scatter_add(tgt, idx, src, axis=0):
    return tgt.at[idx].add(src)

def _segment_sum(src, seg, n):
    return jax.ops.segment_sum(src, seg, n)
kernel_name = 'mk_perceiver_d1_seqx_r4_1ae3d5'

def setup_inputs(seed: int=0):
    np.random.seed(seed)
    _w = jnp.asarray

    def _rec_inputs():
        import jax
        import jax.numpy as jnp
        _rk = jax.random.key(seed)
        x = -0.0002928 + 1 * jax.random.normal(jax.random.fold_in(_rk, 1), (2, 64, 256), jnp.float32)
        _lenS = 64 - jax.random.randint(jax.random.fold_in(_rk, 7), (2,), 0, max(1, 64 // 4) + 1, jnp.int32)
        _lenS2 = 1024 - jax.random.randint(jax.random.fold_in(_rk, 8), (2,), 0, max(1, 1024 // 4) + 1, jnp.int32)
        _ctx_1024P = jax.random.normal(jax.random.fold_in(_rk, 11), (2, 16, 256), jnp.float32)
        _ctx_1024c = jax.random.dirichlet(jax.random.fold_in(_rk, 511), 0.3 * jnp.ones((16,), jnp.float32), (2, 1024))
        _ctx_1024t = jnp.einsum('bsk,bkd->bsd', _ctx_1024c, _ctx_1024P)
        _ctx_1024t = _ctx_1024t * jax.lax.rsqrt(jnp.mean(jnp.square(_ctx_1024t)) + 1e-12) * 0.953939
        ctx_1024 = -1.39393e-06 + 0.999914 * (_ctx_1024t + 0.3 * jax.random.normal(jax.random.fold_in(_rk, 611), (2, 1024, 256), jnp.float32))
        return (x, ctx_1024)
    x, ctx_1024 = _rec_inputs()

    def _L0_xattn_setup():
        import jax, jax.numpy as jnp
        import numpy as np
        B, NQ, NK, D = (2, 512, 512, 256)
        HEADS, DIM_HEAD = (16, 64)
        INNER = HEADS * DIM_HEAD
        DIM_OUT = 256
        key = jax.random.key(seed)
        ks = jax.random.split(key, 8)
        s = lambda fan_in: 1.0 / np.sqrt(fan_in)
        return {'x': jax.random.normal(ks[0], (B, NQ, D), jnp.float32), 'context': jax.random.normal(ks[1], (B, NK, D), jnp.float32), 'Wq': jax.random.normal(ks[2], (D, INNER), jnp.float32) * s(D), 'Wkv': jax.random.normal(ks[3], (D, 2 * INNER), jnp.float32) * s(D), 'null_key': jax.random.normal(ks[4], (DIM_HEAD,), jnp.float32), 'null_value': jax.random.normal(ks[5], (DIM_HEAD,), jnp.float32), 'Wout': jax.random.normal(ks[6], (INNER, DIM_OUT), jnp.float32) * s(INNER), 'bout': jnp.zeros((DIM_OUT,), jnp.float32)}
    _L0_xattn_all = _L0_xattn_setup()
    _L0_xattn_in = {k: v for k, v in _L0_xattn_all.items() if k in ('Wq', 'Wkv', 'null_key', 'null_value', 'Wout', 'bout')}
    del _L0_xattn_all

    def _L0_attn_setup():
        import jax, jax.numpy as jnp
        import numpy as np
        HEADS = 4
        EPS = 1e-05
        GATE_LOGIT_NORMALIZER = 16.0
        B, N, D = (4, 512, 256)
        DK, DV, R = (256, 512, 16)

        def _gla_scan(q, k, v, gk):
            dk, dv = (q.shape[1], v.shape[1])

            def step(S, inp):
                q_t, k_t, v_t, g_t = inp
                S = S * jnp.exp(g_t)[:, None] + k_t[:, None] * v_t[None, :]
                return (S, q_t @ S)
            S0 = jnp.zeros((dk, dv), q.dtype)
            _, o = jax.lax.scan(step, S0, (q, k, v, gk))
            return o
        key = jax.random.key(seed)
        ks = jax.random.split(key, 10)
        s = 0.02
        return {'x': jax.random.normal(ks[0], (B, N, D), jnp.float32), 'Wq': jax.random.normal(ks[1], (D, DK), jnp.float32) * s, 'Wk': jax.random.normal(ks[2], (D, DK), jnp.float32) * s, 'Wv': jax.random.normal(ks[3], (D, DV), jnp.float32) * s, 'Wg': jax.random.normal(ks[4], (D, DV), jnp.float32) * s, 'Wgk1': jax.random.normal(ks[5], (D, R), jnp.float32) * s, 'Wgk2': jax.random.normal(ks[6], (R, DK), jnp.float32) * s, 'bgk2': jnp.zeros((DK,), jnp.float32), 'Wo': jax.random.normal(ks[7], (DV, D), jnp.float32) * s, 'g_norm_weight': jnp.ones((DV // HEADS,), jnp.float32)}
    _L0_attn_all = _L0_attn_setup()
    _L0_attn_in = {k: v for k, v in _L0_attn_all.items() if k in ('Wq', 'Wk', 'Wv', 'Wg', 'Wgk1', 'Wgk2', 'bgk2', 'Wo', 'g_norm_weight')}
    del _L0_attn_all

    def _L0_ffn_setup():
        import jax, jax.numpy as jnp
        import numpy as np
        TOP_K = 2
        CAP_FACTOR = 1.25
        EPS = 1.1920929e-07
        key = jax.random.key(seed)
        ks = jax.random.split(key, 6)
        B, S, D, E, H = (8, 512, 256, 8, 1024)
        return {'hidden_states': jax.random.normal(ks[0], (B, S, D), jnp.float32), 'wg': jax.random.normal(ks[1], (D, E), jnp.float32) * 0.02, 'fc1_w': jax.random.normal(ks[2], (E, H, D), jnp.float32) * 0.02, 'fc1_b': jnp.zeros((E, H), jnp.float32), 'fc2_w': jax.random.normal(ks[3], (E, H, D), jnp.float32) * 0.02, 'fc2_b': jnp.zeros((E, D), jnp.float32), 'ln_gamma': jnp.ones((D,), jnp.float32), 'ln_beta': jnp.zeros((D,), jnp.float32)}
    _L0_ffn_all = _L0_ffn_setup()
    _L0_ffn_in = {k: v for k, v in _L0_ffn_all.items() if k in ('wg', 'fc1_w', 'fc1_b', 'fc2_w', 'fc2_b', 'ln_gamma', 'ln_beta')}
    del _L0_ffn_all
    return {'x': x, 'ctx_1024': ctx_1024, 'L0_xattn_Wq': _L0_xattn_in['Wq'], 'L0_xattn_Wkv': _L0_xattn_in['Wkv'], 'L0_xattn_null_key': _L0_xattn_in['null_key'], 'L0_xattn_null_value': _L0_xattn_in['null_value'], 'L0_xattn_Wout': _L0_xattn_in['Wout'], 'L0_xattn_bout': _L0_xattn_in['bout'], 'L0_attn_Wq': _L0_attn_in['Wq'], 'L0_attn_Wk': _L0_attn_in['Wk'], 'L0_attn_Wv': _L0_attn_in['Wv'], 'L0_attn_Wg': _L0_attn_in['Wg'], 'L0_attn_Wgk1': _L0_attn_in['Wgk1'], 'L0_attn_Wgk2': _L0_attn_in['Wgk2'], 'L0_attn_bgk2': _L0_attn_in['bgk2'], 'L0_attn_Wo': _L0_attn_in['Wo'], 'L0_attn_g_norm_weight': _L0_attn_in['g_norm_weight'], 'L0_ffn_wg': _L0_ffn_in['wg'], 'L0_ffn_fc1_w': _L0_ffn_in['fc1_w'], 'L0_ffn_fc1_b': _L0_ffn_in['fc1_b'], 'L0_ffn_fc2_w': _L0_ffn_in['fc2_w'], 'L0_ffn_fc2_b': _L0_ffn_in['fc2_b'], 'L0_ffn_ln_gamma': _L0_ffn_in['ln_gamma'], 'L0_ffn_ln_beta': _L0_ffn_in['ln_beta']}

def reference(x, ctx_1024, L0_xattn_Wq, L0_xattn_Wkv, L0_xattn_null_key, L0_xattn_null_value, L0_xattn_Wout, L0_xattn_bout, L0_attn_Wq, L0_attn_Wk, L0_attn_Wv, L0_attn_Wg, L0_attn_Wgk1, L0_attn_Wgk2, L0_attn_bgk2, L0_attn_Wo, L0_attn_g_norm_weight, L0_ffn_wg, L0_ffn_fc1_w, L0_ffn_fc1_b, L0_ffn_fc2_w, L0_ffn_fc2_b, L0_ffn_ln_gamma, L0_ffn_ln_beta):
    import jax
    import jax.numpy as jnp

    def _L0_xattn_ref(x, context, Wq, Wkv, null_key, null_value, Wout, bout):
        import jax, jax.numpy as jnp
        import numpy as np
        B, NQ, NK, D = (2, 512, 512, 256)
        HEADS, DIM_HEAD = (16, 64)
        INNER = HEADS * DIM_HEAD
        DIM_OUT = 256
        b = x.shape[0]
        scale = DIM_HEAD ** (-0.5)
        q = x @ Wq
        kv = context @ Wkv
        k, v = jnp.split(kv, 2, axis=-1)
        split_heads = lambda t: t.reshape(t.shape[0], t.shape[1], HEADS, DIM_HEAD).transpose(0, 2, 1, 3)
        q, k, v = map(split_heads, (q, k, v))
        nk = jnp.broadcast_to(null_key, (b, HEADS, 1, DIM_HEAD))
        nv = jnp.broadcast_to(null_value, (b, HEADS, 1, DIM_HEAD))
        k = jnp.concatenate((nk, k), axis=-2)
        v = jnp.concatenate((nv, v), axis=-2)
        q = jnp.tanh(q)
        k = jnp.tanh(k)
        sim = jnp.einsum('bhid,bhjd->bhij', q, k) * scale
        attn = jax.nn.softmax(sim, axis=-1)
        out = jnp.einsum('bhij,bhjd->bhid', attn, v)
        out = out.transpose(0, 2, 1, 3).reshape(b, -1, INNER)
        return out @ Wout + bout

    def _L0_attn_ref(x, Wq, Wk, Wv, Wg, Wgk1, Wgk2, bgk2, Wo, g_norm_weight):
        import jax, jax.numpy as jnp
        import numpy as np
        HEADS = 4
        EPS = 1e-05
        GATE_LOGIT_NORMALIZER = 16.0
        B, N, D = (4, 512, 256)
        DK, DV, R = (256, 512, 16)

        def _gla_scan(q, k, v, gk):
            dk, dv = (q.shape[1], v.shape[1])

            def step(S, inp):
                q_t, k_t, v_t, g_t = inp
                S = S * jnp.exp(g_t)[:, None] + k_t[:, None] * v_t[None, :]
                return (S, q_t @ S)
            S0 = jnp.zeros((dk, dv), q.dtype)
            _, o = jax.lax.scan(step, S0, (q, k, v, gk))
            return o
        b, n, d = x.shape
        h = HEADS
        dk = Wq.shape[1] // h
        dv = Wv.shape[1] // h
        split = lambda t, hd: t.reshape(b, n, h, hd).transpose(0, 2, 1, 3)
        q = split(x @ Wq, dk) * dk ** (-0.5)
        k = split(x @ Wk, dk)
        v = split(x @ Wv, dv)
        gk = jax.nn.log_sigmoid(x @ Wgk1 @ Wgk2 + bgk2) / GATE_LOGIT_NORMALIZER
        gk = split(gk, dk)
        o = jax.vmap(jax.vmap(_gla_scan))(q, k, v, gk)
        o = o.transpose(0, 2, 1, 3)
        g = (x @ Wg).reshape(b, n, h, dv)
        o = o * jax.lax.rsqrt(jnp.mean(o * o, axis=-1, keepdims=True) + EPS) * g_norm_weight
        o = o * (g * jax.nn.sigmoid(g))
        return o.reshape(b, n, h * dv) @ Wo

    def _L0_ffn_ref(hidden_states, wg, fc1_w, fc1_b, fc2_w, fc2_b, ln_gamma, ln_beta):
        import jax, jax.numpy as jnp
        import numpy as np
        TOP_K = 2
        CAP_FACTOR = 1.25
        EPS = 1.1920929e-07
        B, S, D = hidden_states.shape
        E = wg.shape[1]
        N = B * S
        k = TOP_K
        C = k * int(CAP_FACTOR * ((N + E - 1) // E))
        x = hidden_states.reshape(N, D)
        scores = jax.nn.softmax(x @ wg, axis=-1)
        gates, idx = jax.lax.top_k(scores, k)
        gates = gates / jnp.clip(jnp.sum(gates, -1, keepdims=True), EPS)
        masks = jax.nn.one_hot(idx, E, dtype=jnp.int32)
        counts = masks.sum(0)
        offsets = jnp.concatenate([jnp.zeros((1, E), jnp.int32), jnp.cumsum(counts, 0)[:-1]], 0)
        loc = jnp.cumsum(masks, 0) - 1 + offsets[None]
        loc_sel = (loc * masks).sum(-1)
        keep = loc_sel < C
        gates = gates * keep.astype(gates.dtype)
        pos = jnp.where(keep, idx * C + loc_sel, E * C)
        xk = jnp.broadcast_to(x[:, None, :], (N, k, D)).reshape(N * k, D)
        buf = jnp.zeros((E * C + 1, D), x.dtype).at[pos.reshape(-1)].set(xk)
        disp = buf[:E * C].reshape(E, C, D)
        h = jax.nn.silu(jnp.einsum('ecd,ehd->ech', disp, fc1_w) + fc1_b[:, None, :])
        y = jnp.einsum('ech,ehd->ecd', h, fc2_w) + fc2_b[:, None, :]
        ybuf = jnp.concatenate([y.reshape(E * C, D), jnp.zeros((1, D), y.dtype)], 0)
        combined = jnp.sum(gates[..., None] * ybuf[pos], axis=1)
        res = hidden_states + combined.reshape(B, S, D)
        mu = jnp.mean(res, -1, keepdims=True)
        var = jnp.var(res, -1, keepdims=True)
        return (res - mu) * jax.lax.rsqrt(var + 1e-05) * ln_gamma + ln_beta
    x = x + _L0_xattn_ref(_layernorm(x, axis=-1), ctx_1024, L0_xattn_Wq, L0_xattn_Wkv, L0_xattn_null_key, L0_xattn_null_value, L0_xattn_Wout, L0_xattn_bout)
    x = x + _L0_attn_ref(_layernorm(x, axis=-1), L0_attn_Wq, L0_attn_Wk, L0_attn_Wv, L0_attn_Wg, L0_attn_Wgk1, L0_attn_Wgk2, L0_attn_bgk2, L0_attn_Wo, L0_attn_g_norm_weight)
    x = x + _L0_ffn_ref(_layernorm(x, axis=-1), L0_ffn_wg, L0_ffn_fc1_w, L0_ffn_fc1_b, L0_ffn_fc2_w, L0_ffn_fc2_b, L0_ffn_ln_gamma, L0_ffn_ln_beta)
    return x

_drawn_inputs = setup_inputs


def setup_inputs(seed=0):
    import zlib

    import numpy as np

    out = dict(_drawn_inputs(seed))
    spreads = {'L0_xattn_bout': (0.0, 0.1),
     'L0_attn_bgk2': (0.0, 2.0),
     'L0_attn_g_norm_weight': (1.0, 0.6),
     'L0_ffn_fc1_b': (0.0, 0.789),
     'L0_ffn_fc2_b': (0.0, 0.272),
     'L0_ffn_ln_gamma': (1.0, 0.2),
     'L0_ffn_ln_beta': (0.0, 0.1)}
    factors = {'L0_xattn_null_key': 64.0,
     'L0_xattn_null_value': 29.797,
     'L0_attn_Wgk1': 8.0,
     'L0_attn_Wgk2': 8.0}
    for name, (base, spread) in spreads.items():
        noise = np.random.default_rng([zlib.crc32(name.encode()), seed]).standard_normal(out[name].shape)
        drawn = base * np.exp(spread * noise) if base else spread * noise
        out[name] = jnp.asarray(drawn.astype(out[name].dtype))
    for name, factor in factors.items():
        out[name] = (out[name] * factor).astype(out[name].dtype)
    return out
```

```python
from contextlib import ExitStack

import numpy as np

import concourse.bass as bass
from concourse import mybir

F32 = mybir.dt.float32
F32R = mybir.dt.float32r
U32 = mybir.dt.uint32
ALU = mybir.AluOpType
ACT = mybir.ActivationFunctionType
AX = mybir.AxisListType

P = 128
B, S, D = 2, 64, 256
NK = 1024
H, DH = 16, 64
INNER = H * DH
DC = D // P
CK = 512
NC = NK // CK
KT = CK // P
G = 2
HG = H // G
PG = HG // 2
NPAIR = H // 2
LH, LDK, LDV, LR = 4, 64, 128, 16
LEVELS = [32, 16, 8, 4, 2, 1]
NL = len(LEVELS)
GATE_NORM = 16.0
E, FH = 8, 1024
FC = FH // P
N_TOK = B * S
CAP = 2 * int(1.25 * ((N_TOK + E - 1) // E))
SLOTS = 64
LN_EPS = 1e-5
GATE_EPS = 1.1920929e-07
assert B * S == P and CAP <= SLOTS

C_EYE, C_STRICT, C_ONES, C_IOTA8, C_ROWONE, C_MASK, C_DECAY, C_SLOT = 0, 128, 256, 384, 392, 400, 784, 1552
C_WIDTH = C_SLOT + E * SLOTS


def shape_constants():
    c = np.zeros((P, C_WIDTH), np.float32)
    t = np.arange(P)
    c[:, C_EYE:C_EYE + P] = np.eye(P)
    c[:, C_STRICT:C_STRICT + P] = t[:, None] < t[None, :]
    c[:, C_ONES:C_ONES + P] = 1.0
    c[:, C_IOTA8:C_IOTA8 + E] = np.arange(E)
    c[:, C_ROWONE] = LN_EPS
    c[:, C_ROWONE + 1] = -0.5
    for n, half in enumerate(LEVELS):
        block, right = t // (2 * half), t // half % 2 == 1
        edge = block * 2 * half + half
        cols = t[right]
        same = block[:, None] == block[None, cols]
        c[:, C_MASK + n * 64:C_MASK + (n + 1) * 64] = same & ~right[:, None]
        u, at = t[:, None], t[None, :]
        in_right = (u >= edge[None, :]) & (u <= at)
        in_left = (u > at) & (u < edge[None, :])
        c[:, C_DECAY + n * P:C_DECAY + (n + 1) * P] = np.where(right[None, :], in_right, in_left)
    c[:, C_SLOT:] = np.arange(1, E * SLOTS + 1)
    return c


def block_kernel(nc, a, out):
    with ExitStack() as whole:
        def sem(name):
            return whole.enter_context(nc.semaphore(name))

        def alloc(stack, name, shape, dt=F32):
            return stack.enter_context(nc.sbuf_tensor(name, shape, dt))

        ps = whole.enter_context(nc.psum_tensor("ps", [P, 8, 512], F32))

        def keep(name, shape, dt=F32):
            return alloc(whole, name, shape, dt)

        const = keep("const", [P, C_WIDTH])
        eye = const[:, C_EYE:C_EYE + P]
        strict = const[:, C_STRICT:C_STRICT + P]
        ones = const[:, C_ONES:C_ONES + P]
        iota8 = const[:, C_IOTA8:C_IOTA8 + E]
        minus_half = const[:, C_ROWONE + 1:C_ROWONE + 2]
        slot_no = const[:, C_SLOT:C_SLOT + E * SLOTS]
        x0 = keep("x0", [P, D])
        x1 = keep("x1", [P, D])
        x2 = keep("x2", [P, D])
        xn = keep("xn", [P, D])
        xnT = keep("xnT", [P, DC, P])
        bout = keep("bout", [P, D])
        gamma = keep("gamma", [P, D])
        beta = keep("beta", [P, D])
        gnorm = keep("gnorm", [P, LDV])
        stat = keep("stat", [P, 4, 16])
        w_lq = keep("w_lq", [P, DC, LH * LDK])
        w_lk = keep("w_lk", [P, DC, LH * LDK])
        w_lv = keep("w_lv", [P, DC, LH * LDV])
        w_lg = keep("w_lg", [P, DC, LH * LDV])
        w_lo = keep("w_lo", [P, LH, D])
        w_gk1 = keep("w_gk1", [P, DC, LR])
        w_gk2 = keep("w_gk2", [32, LH * LDK])
        w_route = keep("w_route", [P, DC, E])
        b1 = keep("b1", [P, E, FC])
        b2 = keep("b2", [P, E // 2, D])

        attn_a = ExitStack()
        ctxT_h = alloc(attn_a, "ctxT_h", [P, 2, DC, CK], F32R)
        ctxT_l = alloc(attn_a, "ctxT_l", [P, 2, DC, CK], F32R)
        w_k_h = alloc(attn_a, "w_k_h", [P, DC, INNER], F32R)
        w_k_l = alloc(attn_a, "w_k_l", [P, DC, INNER], F32R)
        stage_t = alloc(attn_a, "stage_t", [P, 2, DC, CK])
        stage_n = alloc(attn_a, "stage_n", [P, 2, KT, D])
        keys = alloc(attn_a, "keys", [P, 2 * PG, CK])
        ctx_h = alloc(attn_a, "ctx_h", [P, 2, KT, D], F32R)
        ctx_l = alloc(attn_a, "ctx_l", [P, 2, KT, D], F32R)
        NE = 4
        ex = alloc(attn_a, "ex", [P, NE, CK])
        ex_h = alloc(attn_a, "ex_h", [P, NE, CK], F32R)
        ex_l = alloc(attn_a, "ex_l", [P, NE, CK], F32R)
        q_blk = alloc(attn_a, "q_blk", [P, NPAIR, B, P])
        attn_b = ExitStack()
        w_v = alloc(attn_b, "w_v", [P, DC, INNER])
        w_out = alloc(attn_b, "w_out", [P, FC, D])
        mixT = alloc(attn_b, "mixT", [P, DC, H, B, S])
        ex_sum = alloc(attn_b, "ex_sum", [P, H, B, S])
        w_q = mixT[:, 0].rearrange("p h b s -> p (h b s)").rearrange("p (c n) -> p c n", c=DC)
        null_v = alloc(attn_b, "null_v", [H, INNER])
        null_k = alloc(attn_b, "null_k", [P, NPAIR, H])
        null_kt = alloc(attn_b, "null_kt", [P, NPAIR, H])
        null_ex = alloc(attn_b, "null_ex", [H, P])
        qT = alloc(attn_b, "qT", [P, NPAIR, P])
        mixed = alloc(attn_b, "mixed", [P, INNER])
        mixedT = alloc(attn_b, "mixedT", [P, FC, P])
        den = alloc(attn_b, "den", [P, H])
        w_k_stage = keys[:, 2 * PG - 4:2 * PG, :].rearrange("p (g c) n -> p g c n", g=G)
        attn_b.close()
        attn_a.close()

        w1, w2 = [], []
        for e in range(E):
            w1.append(keep(f"w1_{e}", [P, DC, FH]))
            w2.append(keep(f"w2_{e}", [P, FC, D]))

        lin = ExitStack()
        lqT = alloc(lin, "lqT", [P, 2, 2, P])
        lkT = alloc(lin, "lkT", [P, 2, P])
        lowT = alloc(lin, "lowT", [32, P])
        gate = alloc(lin, "gate", [P, 4, LH * LDK])
        lv = alloc(lin, "lv", [P, LH * LDV])
        silu = alloc(lin, "silu", [P, 2, LH * LDV])
        decay = alloc(lin, "decay", [P, 2, NL, P])
        kx = alloc(lin, "kx", [P, 2, NL, P])
        qx = alloc(lin, "qx", [P, 2, 2, NL, 64])
        att = alloc(lin, "att", [P, LH, P])
        lo = alloc(lin, "lo", [P, 3, LH * LDV])
        loT = alloc(lin, "loT", [P, LH, P])
        lstat = alloc(lin, "lstat", [P, 4, LH])
        lin.close()

        moe = whole
        rt = alloc(moe, "rt", [P, 16, 8])
        rt_idx = alloc(moe, "rt_idx", [P, 8], U32)
        pick = alloc(moe, "pick", [P, 2, E])
        onehot = alloc(moe, "onehot", [P, E * SLOTS])
        gated = alloc(moe, "gated", [P, E * SLOTS])
        gatedT = alloc(moe, "gatedT", [P, E // 2, P])
        xd = alloc(moe, "xd", [P, DC, E * SLOTS])
        hid = alloc(moe, "hid", [P, FH])
        hu = alloc(moe, "hu", [P, FC, 2, CAP])
        ht = alloc(moe, "ht", [P, FC, 2, CAP])
        hT = alloc(moe, "hT", [P, 2, FC, 2, SLOTS])
        ysb = alloc(moe, "ysb", [P, 2, D])
        fin = alloc(moe, "fin", [P, 3, D])

        ld_x = sem("ld_x")
        ld_const = sem("ld_const")
        ld_wq = sem("ld_wq")
        ld_wk = [sem(f"ld_wk{g}") for g in range(G)]
        ld_ctx = [sem(f"ld_ctx{n}") for n in range(B * NC)]
        ld_null = sem("ld_null")
        ld_wv = sem("ld_wv")
        ld_lin = sem("ld_lin")
        ld_small = sem("ld_small")
        ld_exp = [sem(f"ld_exp{e}") for e in range(E)]
        st_out = sem("st_out")
        dve_seq = sem("dve_seq")
        act_seq = sem("act_seq")
        var_ready = sem("var_ready")
        rstd_ready = sem("rstd_ready")
        xn_ready = sem("xn_ready")
        xnT_psum = sem("xnT_psum")
        xnT_ready = sem("xnT_ready")
        zero_ready = sem("zero_ready")
        q_psum = sem("q_psum")
        q_tanh = sem("q_tanh")
        q_ready = sem("q_ready")
        nk_tanh = sem("nk_tanh")
        null_psum = sem("null_psum")
        null_ready = sem("null_ready")
        wk_high = sem("wk_high")
        wk_ready = sem("wk_ready")
        ctxT_high = sem("ctxT_high")
        ctxT_ready = sem("ctxT_ready")
        ctx_ready = sem("ctx_ready")
        k_psum = sem("k_psum")
        k_ready = sem("k_ready")
        s_psum = sem("s_psum")
        e_ready = sem("e_ready")
        el_ready = sem("el_ready")
        esum_ready = sem("esum_ready")
        mix_done = sem("mix_done")
        mixT_ready = sem("mixT_ready")
        den_psum = sem("den_psum")
        o_psum = sem("o_psum")
        o_ready = sem("o_ready")
        oT_psum = sem("oT_psum")
        oT_ready = sem("oT_ready")
        wo_psum = sem("wo_psum")
        x1_ready = sem("x1_ready")
        low_psum = sem("low_psum")
        low_ready = sem("low_ready")
        logit_psum = sem("logit_psum")
        qk_psum = sem("qk_psum")
        qk_ready = sem("qk_ready")
        v_psum = sem("v_psum")
        v_ready = sem("v_ready")
        g_psum = sem("g_psum")
        gln_ready = sem("gln_ready")
        g_ready = sem("g_ready")
        dec_psum = sem("dec_psum")
        dec_ready = sem("dec_ready")
        gtanh_ready = sem("gtanh_ready")
        kx_ready = sem("kx_ready")
        qx_ready = sem("qx_ready")
        lev_psum = sem("lev_psum")
        att_ready = sem("att_ready")
        lo_psum = sem("lo_psum")
        sq_ready = sem("sq_ready")
        ms_ready = sem("ms_ready")
        lr_ready = sem("lr_ready")
        lo_ready = sem("lo_ready")
        loT_psum = sem("loT_psum")
        loT_ready = sem("loT_ready")
        lw_psum = sem("lw_psum")
        x2_ready = sem("x2_ready")
        rl_psum = sem("rl_psum")
        rd_ready = sem("rd_ready")
        rexp_ready = sem("rexp_ready")
        pick_ready = sem("pick_ready")
        loc_psum = sem("loc_psum")
        oh_ready = sem("oh_ready")
        xd_psum = sem("xd_psum")
        xd_ready = sem("xd_ready")
        gated_ready = sem("gated_ready")
        gatedT_psum = sem("gatedT_psum")
        gatedT_ready = sem("gatedT_ready")
        f1_psum = sem("f1_psum")
        hid_ready = sem("hid_ready")
        hidT_psum = sem("hidT_psum")
        hu_ready = sem("hu_ready")
        ht_ready = sem("ht_ready")
        hT_ready = sem("hT_ready")
        y_psum = sem("y_psum")
        y_ready = sem("y_ready")
        c_psum = sem("c_psum")
        out_ready = sem("out_ready")

        units = [(b, c, g) for b in range(B) for c in range(NC) for g in range(G)]
        NU = len(units)
        STEPS = NU * KT

        def mix_bank(half, g):
            return 2 * half + g
        K_BANK, S_BANK = 4, 6

        block = whole.enter_context(nc.Block())

        @block.sync
        def _(sp):
            def load_chunk(n):
                b, c = n // NC, n % NC
                if n >= 2:
                    sp.wait_ge(ctx_ready, n - 1)
                cols = slice(b * NK + c * CK, b * NK + (c + 1) * CK)
                sp.dma_start(stage_t[:, n % 2], a["ctxT"][:, cols].rearrange("(c p) n -> p c n", p=P)).then_inc(ld_ctx[n], 16)
                sp.dma_start(stage_n[:, n % 2], a["ctx"][cols, :].rearrange("(t p) d -> p t d", p=P)).then_inc(ld_ctx[n], 16)

            def load_wk(g):
                sp.dma_start(w_k_stage[:, g],
                             a["Wkv"][:, g * 512:(g + 1) * 512].rearrange("(c p) n -> p c n", p=P)).then_inc(ld_wk[g], 16)

            def chunked(name, p=P):
                return a[name].rearrange("(c p) n -> p c n", p=p)

            def rows(name, n=P):
                return a[name].rearrange("(o d) -> o d", o=1).broadcast_to([n, a[name].shape[0]])

            sp.dma_start(x0[:], a["x"]).then_inc(ld_x, 16)
            load_wk(0)
            sp.dma_start(const[:], a["const"]).then_inc(ld_const, 16)
            load_chunk(0)
            sp.dma_start(w_q, chunked("Wq")).then_inc(ld_wq, 16)
            load_wk(1)
            sp.dma_start(null_v[:], a["null_v"]).then_inc(ld_null, 16)
            sp.dma_start(null_k[:], a["null_k"]).then_inc(ld_null, 16)
            load_chunk(1)
            sp.dma_start(bout[:], rows("bout")).then_inc(ld_small, 16)
            sp.dma_start(gamma[:], rows("gamma")).then_inc(ld_small, 16)
            sp.dma_start(beta[:], rows("beta")).then_inc(ld_small, 16)
            sp.dma_start(gnorm[:], rows("gnorm")).then_inc(ld_small, 16)
            sp.dma_start(b1[:], a["b1"]).then_inc(ld_small, 16)
            for e in range(E):
                half = SLOTS * (e % 2)
                sp.dma_start(b2[half:half + SLOTS, e // 2, :],
                             a["b2"][e:e + 1, :].broadcast_to([SLOTS, D])).then_inc(ld_small, 16)
            sp.dma_start(w_v[:], a["Wkv"][:, INNER:2 * INNER].rearrange("(c p) n -> p c n", p=P)).then_inc(ld_wv, 16)
            sp.dma_start(w_out[:], chunked("Wout")).then_inc(ld_wv, 16)
            load_chunk(2)
            sp.dma_start(w_lq[:], chunked("lWq")).then_inc(ld_lin, 16)
            sp.dma_start(w_lk[:], chunked("lWk")).then_inc(ld_lin, 16)
            sp.dma_start(w_lv[:], chunked("lWv")).then_inc(ld_lin, 16)
            sp.dma_start(w_lg[:], chunked("lWg")).then_inc(ld_lin, 16)
            sp.dma_start(w_lo[:], chunked("lWo")).then_inc(ld_lin, 16)
            sp.dma_start(w_gk1[:], chunked("Wgk1")).then_inc(ld_lin, 16)
            sp.dma_start(w_gk2[0:LR + 1], a["Wgk2b"]).then_inc(ld_lin, 16)
            sp.dma_start(w_route[:], chunked("wg")).then_inc(ld_lin, 16)
            load_chunk(3)
            for e in range(E):
                if e == 0:
                    sp.wait_ge(k_psum, STEPS)
                if e == 2:
                    sp.wait_ge(ctx_ready, B * NC)
                if e == 3:
                    sp.wait_ge(s_psum, STEPS)
                if e == 4:
                    sp.wait_ge(mix_done, STEPS)
                    sp.wait_ge(esum_ready, STEPS)
                if e == 7:
                    sp.wait_ge(wo_psum, 1)
                sp.dma_start(w1[e][:], a["fc1T"][e].rearrange("(c p) n -> p c n", p=P)).then_inc(ld_exp[e], 16)
                sp.dma_start(w2[e][:], a["fc2"][e].rearrange("(c p) n -> p c n", p=P)).then_inc(ld_exp[e], 16)
            sp.wait_ge(out_ready, 1)
            sp.dma_start(out, fin[:, 2, :]).then_inc(st_out, 16)
            sp.wait_ge(st_out, 16)

        @block.gpsimd
        def _(pool):
            nc.gpsimd.memset(q_blk[:], 0.0).then_inc(zero_ready, 1)
            pool.wait_ge(ld_const, 16)
            for n in range(3):
                pool.wait_ge(var_ready, n + 1)
                nc.gpsimd.tensor_tensor(stat[:, n, 9:10], stat[:, n, 8:9], minus_half, ALU.pow).then_inc(rstd_ready, 1)
                if n == 0:
                    pool.wait_ge(wo_psum, 1)
                    nc.gpsimd.memset(lowT[:], 1.0).then_inc(zero_ready, 1)
                    nc.gpsimd.memset(lqT[:], 0.0).then_inc(zero_ready, 1)
                if n == 1:
                    pool.wait_ge(ms_ready, 1)
                    nc.gpsimd.tensor_tensor(lstat[:, 2], lstat[:, 1], minus_half.broadcast_to([P, LH]),
                                            ALU.pow).then_inc(lr_ready, 1)
                    pool.wait_ge(lw_psum, 1)
                    nc.gpsimd.memset(hT[:], 0.0).then_inc(zero_ready, 1)
            pool.wait_ge(var_ready, 4)
            nc.gpsimd.tensor_tensor(stat[:, 3, 9:10], stat[:, 3, 8:9], minus_half, ALU.pow).then_inc(rstd_ready, 1)

        @block.scalar
        def _(act):
            seq = [0]

            def link(ins):
                seq[0] += 1
                ins.then_inc(act_seq, 1)
                act.wait_ge(act_seq, seq[0])

            def copy(dst, src, done):
                nc.scalar.activation(dst, src, ACT.Copy).then_inc(done, 1)

            def split_wk(g):
                act.wait_ge(ld_wk[g], 16)
                copy(w_k_h[:, :, g * 512:(g + 1) * 512], w_k_stage[:, g], wk_high)

            def keys_tanh(kp):
                u = kp // PG
                act.wait_ge(k_psum, kp + 1)
                if kp == PG:
                    act.wait_ge(wk_ready, G)
                if u >= 2:
                    act.wait_ge(s_psum, KT * (u - 1))
                nc.scalar.activation(keys[:, kp % (2 * PG)], ps[:, K_BANK + kp % 2], ACT.Tanh).then_inc(k_ready, 1)

            split_wk(0)
            act.wait_ge(ld_ctx[0], 32)
            copy(ctxT_h[:, 0], stage_t[:, 0], ctxT_high)
            split_wk(1)
            act.wait_ge(ld_null, 32)
            nc.scalar.activation(null_kt[:], null_k[:], ACT.Tanh).then_inc(nk_tanh, 1)
            for j in range(2):
                act.wait_ge(q_psum, j + 1)
                nc.scalar.activation(qT[:, 4 * j:4 * j + 4], ps[:, 1 + j].rearrange("p (j t) -> p j t", t=P),
                                     ACT.Tanh).then_inc(q_tanh, 1)
                for kp in range(2 * j, 2 * j + 2):
                    keys_tanh(kp)
            act.wait_ge(null_psum, 1)
            nc.scalar.activation(null_ex[:], ps[0:H, 3, 0:P], ACT.Exp, scale=DH ** -0.5).then_inc(null_ready, 1)

            for s in range(STEPS):
                act.wait_ge(s_psum, s + 1)
                r = s % NE
                if s >= NE:
                    act.wait_ge(esum_ready, s - NE + 1)
                    act.wait_ge(mix_done, s - NE + 1)
                nc.scalar.activation(ex[:, r], ps[:, S_BANK + s % 2], ACT.Exp, scale=DH ** -0.5)
                nc.scalar.activation(ex_h[:, r], ps[:, S_BANK + s % 2], ACT.Exp, scale=DH ** -0.5).then_inc(e_ready, 1)
                if s + KT < STEPS:
                    keys_tanh(s + KT)
            act.preload_act_table_set("natural_log_exp_and_others")
            for g in range(G):
                act.wait_ge(oT_psum, g + 1)
                copy(mixedT[:, 4 * g:4 * g + 4], ps[:, 0].rearrange("p (c t) -> p c t", t=P), oT_ready)

            act.wait_ge(xnT_psum, 2)
            copy(xnT[:], ps[:, 0, 0:DC * P].rearrange("p (c t) -> p c t", c=DC), xnT_ready)
            act.wait_ge(logit_psum, 1)
            link(nc.scalar.activation(gate[:, 0], ps[:, 3, 0:D], ACT.Abs))
            link(nc.scalar.activation(gate[:, 1], gate[:, 0], ACT.Exp, scale=-1.0))
            nc.scalar.activation(gate[:, 2], gate[:, 1], ACT.Ln, bias=1.0).then_inc(gln_ready, 1)
            act.preload_act_table_set("exp_and_others")
            act.wait_ge(v_psum, 1)
            copy(lv[:], ps[:, 4], v_ready)
            for pair in range(2):
                act.wait_ge(dec_psum, pair + 1)
                bank = (6, 2)[pair]
                src = ps[:, bank:bank + 2, :].rearrange("p a n -> p (a n)")[:, 0:NL * P]
                nc.scalar.activation(decay[:, pair].rearrange("p l t -> p (l t)"), src, ACT.Exp,
                                     scale=1.0 / GATE_NORM).then_inc(dec_ready, 1)
            act.wait_ge(g_psum, 1)
            nc.scalar.activation(silu[:, 0], ps[:, 5], ACT.Tanh, scale=0.5).then_inc(gtanh_ready, 1)
            act.wait_ge(lo_psum, 1)
            nc.scalar.activation(lo[:, 0], ps[:, 2], ACT.Square).then_inc(sq_ready, 1)
            act.wait_ge(loT_psum, 1)
            copy(loT[:], ps[:, 3].rearrange("p (c t) -> p c t", t=P), loT_ready)

            act.wait_ge(xnT_psum, 3)
            copy(xnT[:], ps[:, 0, 0:DC * P].rearrange("p (c t) -> p c t", c=DC), xnT_ready)
            act.wait_ge(rd_ready, 1)
            nc.scalar.activation(rt[:, 2], rt[:, 1], ACT.Exp, accum_out=rt[:, 3, 0:1]).then_inc(rexp_ready, 1)
            act.wait_ge(xd_psum, 2)
            copy(xd[:, 1], ps[:, 5], xd_ready)
            for n in range(E // 2):
                for half in range(2):
                    act.wait_ge(f1_psum, 2 * n + half + 1)
                    if n >= 1:
                        act.wait_ge(hidT_psum, 2 * (n - 1) + half + 1)
                    copy(hid[:, half * 512:(half + 1) * 512], ps[:, half], hid_ready)
                for half in range(2):
                    act.wait_ge(hu_ready, 2 * n + half + 1)
                    if n >= 1:
                        act.wait_ge(hT_ready, 2 * (n - 1) + half + 1)
                    nc.scalar.activation(ht[:, 4 * half:4 * half + 4], hu[:, 4 * half:4 * half + 4], ACT.Tanh,
                                         scale=0.5).then_inc(ht_ready, 1)
                if n == 0:
                    act.wait_ge(gatedT_psum, 1)
                    copy(gatedT[:], ps[:, 3].rearrange("p (n t) -> p n t", t=P), gatedT_ready)

        @block.vector
        def _(dve):
            V = nc.vector
            seq = [0]

            def link(ins):
                seq[0] += 1
                ins.then_inc(dve_seq, 1)
                dve.wait_ge(dve_seq, seq[0])

            def norm_stats(n, src):
                link(V.bn_stats(stat[:, n, 0:6], src))
                link(V.bn_aggr(stat[:, n, 6:8], stat[:, n, 0:6]))
                V.tensor_scalar(stat[:, n, 8:9], stat[:, n, 7:8], LN_EPS, None, ALU.add).then_inc(var_ready, 1)

            def normalise(n, dst, src):
                dve.wait_ge(rstd_ready, n + 1)
                return V.tensor_scalar(dst, src, stat[:, n, 6:7], stat[:, n, 9:10], ALU.subtract, ALU.mult)

            def low_part(dst, full, high):
                return V.tensor_tensor(dst, full, high.bitcast(F32), ALU.subtract)

            def split_wk(g):
                dve.wait_ge(wk_high, g + 1)
                cols = slice(g * 512, (g + 1) * 512)
                low_part(w_k_l[:, :, cols], w_k_stage[:, g], w_k_h[:, :, cols]).then_inc(wk_ready, 1)

            def split_ctxT(n):
                r = n % 2
                if n == 0:
                    dve.wait_ge(ctxT_high, 1)
                else:
                    dve.wait_ge(ld_ctx[n], 32)
                    if n >= 2:
                        dve.wait_ge(k_psum, G * PG * (n - 1))
                    link(V.tensor_copy(ctxT_h[:, r], stage_t[:, r]))
                low_part(ctxT_l[:, r], stage_t[:, r], ctxT_h[:, r]).then_inc(ctxT_ready, 1)

            def split_ctx(n):
                r = n % 2
                dve.wait_ge(ld_ctx[n], 32)
                if n >= 2:
                    dve.wait_ge(mix_done, G * KT * (n - 1))
                link(V.tensor_copy(ctx_h[:, r], stage_n[:, r]))
                low_part(ctx_l[:, r], stage_n[:, r], ctx_h[:, r]).then_inc(ctx_ready, 1)

            def evacuate(u):
                b, c, g = units[u]
                dve.wait_ge(mix_done, KT * (u + 1))
                for half in range(DC):
                    V.tensor_copy(mixT[:, half, HG * g:HG * (g + 1), b, :],
                                  ps[:, mix_bank(half, g)].rearrange("p (h q) -> p h q", q=S)).then_inc(mixT_ready, 1)

            dve.wait_ge(ld_x, 16)
            norm_stats(0, x0[:])
            normalise(0, xn[:], x0[:]).then_inc(xn_ready, 1)
            split_wk(0)
            split_ctxT(0)
            dve.wait_ge(xnT_psum, 1)
            V.tensor_copy(xnT[:], ps[:, 0, 0:DC * P].rearrange("p (c t) -> p c t", c=DC)).then_inc(xnT_ready, 1)
            split_wk(1)
            for j in range(2):
                dve.wait_ge(q_tanh, j + 1)
                dve.wait_ge(zero_ready, 1)
                for r in range(2):
                    V.tensor_copy(q_blk[64 * r:64 * r + 64, 4 * j:4 * j + 4, :, S * r:S * r + S],
                                  qT[64 * r:64 * r + 64, 4 * j:4 * j + 4].rearrange("p j (b q) -> p j b q", b=B)
                                  ).then_inc(q_ready, 1)
            split_ctx(0)
            dve.wait_ge(ld_small, 16 * (5 + E))
            V.tensor_tensor(x1[:], x0[:], bout[:], ALU.add).then_inc(x1_ready, 1)

            for s in range(STEPS):
                u, t = divmod(s, KT)
                b, c, g = units[u]
                r = s % NE
                dve.wait_ge(e_ready, s + 1)
                if s >= NE:
                    dve.wait_ge(mix_done, s - NE + 1)
                low_part(ex_l[:, r], ex[:, r], ex_h[:, r]).then_inc(el_ready, 1)
                total = ex_sum[:, HG * g:HG * (g + 1), b, :]
                tile = ex[:, r].rearrange("p (h q) -> p h q", q=S)
                if c == 0 and t == 0:
                    V.tensor_copy(total, tile).then_inc(esum_ready, 1)
                else:
                    dve.wait_ge(esum_ready, s)
                    V.tensor_tensor(total, total, tile, ALU.add).then_inc(esum_ready, 1)
                n = b * NC + c
                if g == 0 and n + 1 < B * NC:
                    if t == 1:
                        split_ctxT(n + 1)
                if g == 1 and n + 1 < B * NC and t == 2:
                    split_ctx(n + 1)
                if t == 2 and u >= 1 and units[u - 1][1] == NC - 1:
                    evacuate(u - 1)
            def finish_group(g):
                dve.wait_ge(den_psum, g + 1)
                cols = slice(HG * g, HG * (g + 1))
                bank = (5, 6)[g]
                link(V.reciprocal(den[:, cols], ps[:, bank, 0:HG]))
                dve.wait_ge(o_psum, g + 1)
                V.tensor_tensor(mixed[:, 512 * g:512 * (g + 1)].rearrange("p (h d) -> p h d", d=DH),
                                ps[:, K_BANK + g].rearrange("p (h d) -> p h d", d=DH),
                                den[:, cols].unsqueeze(2).broadcast_to([P, HG, DH]), ALU.mult).then_inc(o_ready, 1)

            finish_group(0)
            evacuate(NU - 1)
            finish_group(1)
            dve.wait_ge(wo_psum, 1)
            dve.wait_ge(x1_ready, 1)
            link(V.tensor_tensor(x1[:], x1[:], ps[:, 1, 0:D], ALU.add))

            norm_stats(1, x1[:])
            normalise(1, xn[:], x1[:]).then_inc(xn_ready, 1)
            dve.wait_ge(low_psum, 1)
            dve.wait_ge(zero_ready, 3)
            V.tensor_copy(lowT[0:LR], ps[0:LR, 2, 0:P]).then_inc(low_ready, 1)
            dve.wait_ge(qk_psum, 1)
            qk = ps[:, 1].rearrange("p (w j t) -> p w j t", w=2, j=2)
            for r in range(2):
                rows = slice(64 * r, 64 * r + 64)
                V.tensor_scalar(lqT[rows, :, r, :], qk[rows, 0], LDK ** -0.5, None, ALU.mult).then_inc(qk_ready, 1)
            V.tensor_copy(lkT[:], qk[:, 1]).then_inc(qk_ready, 1)
            dve.wait_ge(gln_ready, 1)
            V.scalar_tensor_tensor(out=gate[:, 3], in0=ps[:, 3, 0:D], scalar=0.0, in1=gate[:, 2], op0=ALU.min,
                                   op1=ALU.subtract).then_inc(g_ready, 1)
            dve.wait_ge(qk_ready, 3)
            for pair in range(2):
                dve.wait_ge(dec_ready, pair + 1)
                V.tensor_tensor(kx[:, pair], decay[:, pair],
                                lkT[:, pair].unsqueeze(1).broadcast_to([P, NL, P]), ALU.mult).then_inc(kx_ready, 1)
                for n, half in enumerate(LEVELS):
                    right = lqT[:, pair].rearrange("p r (m w l) -> p r m w l", w=2, l=half)[:, :, :, 1, :]
                    dec = decay[:, pair, n].rearrange("p (m w l) -> p m w l", w=2, l=half)[:, :, 1, :]
                    dec = dec.unsqueeze(1).broadcast_to([P, 2, 64 // half, half])
                    V.tensor_tensor(qx[:, pair, :, n].rearrange("p r (m l) -> p r m l", l=half), right, dec,
                                    ALU.mult).then_inc(qx_ready, 1)
            dve.wait_ge(lev_psum, 1)
            link(V.tensor_tensor(att[:], ps[:, 0].rearrange("p (h t) -> p h t", t=P),
                                 eye.unsqueeze(1).broadcast_to([P, LH, P]), ALU.mult))
            for n, half in enumerate(LEVELS):
                dve.wait_ge(lev_psum, 2 + n // 2)
                src = ps[:, (1, 6, 7)[n // 2], 256 * (n % 2):256 * (n % 2) + 256].rearrange("p (h m l) -> p h m l", h=LH, l=half)
                mask = const[:, C_MASK + 64 * n:C_MASK + 64 * n + 64].bitcast(U32).rearrange("p (m l) -> p m l", l=half)
                mask = mask.unsqueeze(1).broadcast_to([P, LH, 64 // half, half])
                dst = att[:].rearrange("p h (m w l) -> p h m w l", w=2, l=half)[:, :, :, 1, :]
                ins = V.copy_predicated(dst, mask, src)
                if n + 1 < NL:
                    link(ins)
                else:
                    ins.then_inc(att_ready, 1)
            dve.wait_ge(gtanh_ready, 1)
            link(V.scalar_tensor_tensor(out=silu[:, 1], in0=silu[:, 0], scalar=1.0, in1=ps[:, 5], op0=ALU.add,
                                        op1=ALU.mult))
            V.scalar_tensor_tensor(out=lo[:, 1].rearrange("p (h d) -> p h d", d=LDV),
                                   in0=silu[:, 1].rearrange("p (h d) -> p h d", d=LDV), scalar=0.5,
                                   in1=gnorm[:].unsqueeze(1).broadcast_to([P, LH, LDV]), op0=ALU.mult,
                                   op1=ALU.mult).then_inc(v_ready, 1)
            dve.wait_ge(sq_ready, 1)
            link(V.tensor_reduce(lstat[:, 0], lo[:, 0].rearrange("p (h d) -> p h d", d=LDV), AX.X, ALU.add))
            V.tensor_scalar(lstat[:, 1], lstat[:, 0], 1.0 / LDV, LN_EPS, ALU.mult, ALU.add).then_inc(ms_ready, 1)
            dve.wait_ge(lr_ready, 1)
            link(V.tensor_tensor(lo[:, 2].rearrange("p (h d) -> p h d", d=LDV),
                                 ps[:, 2].rearrange("p (h d) -> p h d", d=LDV),
                                 lstat[:, 2].unsqueeze(2).broadcast_to([P, LH, LDV]), ALU.mult))
            dve.wait_ge(v_ready, 2)
            V.tensor_tensor(lo[:, 0], lo[:, 2], lo[:, 1], ALU.mult).then_inc(lo_ready, 1)
            dve.wait_ge(lw_psum, 1)
            link(V.tensor_tensor(x2[:], x1[:], ps[:, 4, 0:D], ALU.add))

            norm_stats(2, x2[:])
            normalise(2, xn[:], x2[:]).then_inc(xn_ready, 1)
            V.tensor_tensor(x2[:], x2[:], beta[:], ALU.add).then_inc(x2_ready, 1)
            dve.wait_ge(rl_psum, 1)
            logits = ps[:, 1, 0:E]
            link(V.max(rt[:, 0], logits))
            link(V.max_index(rt_idx[:], rt[:, 0], logits))
            V.tensor_scalar(rt[:, 1], rt[:, 0], rt[:, 0, 0:1], None, ALU.subtract).then_inc(rd_ready, 1)
            idx = rt[:, 4, 0:2]
            link(V.tensor_copy(idx, rt_idx[:, 0:2]))
            for k in range(2):
                V.tensor_scalar(pick[:, k], iota8, rt[:, 4, k:k + 1], None, ALU.is_equal).then_inc(pick_ready, 1)
            dve.wait_ge(loc_psum, 1)
            dve.wait_ge(pick_ready, 2)
            taken = rt[:, 5:7]
            link(V.tensor_tensor(taken, ps[:, 2, 0:2 * E].rearrange("p (k e) -> p k e", k=2), pick[:], ALU.mult))
            link(V.tensor_reduce(rt[:, 7, 0:2], taken, AX.X, ALU.add))
            link(V.tensor_scalar(rt[:, 8, 0:2], rt[:, 7, 0:2], float(CAP), None, ALU.is_lt))
            link(V.scalar_tensor_tensor(out=rt[:, 9, 0:2], in0=idx, scalar=float(SLOTS), in1=rt[:, 7, 0:2],
                                        op0=ALU.mult, op1=ALU.add))
            link(V.scalar_tensor_tensor(out=rt[:, 10, 0:2], in0=rt[:, 9, 0:2], scalar=1.0, in1=rt[:, 8, 0:2],
                                        op0=ALU.add, op1=ALU.mult))
            slot = [rt[:, 10, k:k + 1] for k in range(2)]
            link(V.tensor_scalar(onehot[:], slot_no, slot[0], None, ALU.is_equal))
            V.scalar_tensor_tensor(out=onehot[:], in0=slot_no, scalar=slot[1], in1=onehot[:], op0=ALU.is_equal,
                                   op1=ALU.add).then_inc(oh_ready, 1)
            dve.wait_ge(rexp_ready, 1)
            link(V.reciprocal(rt[:, 3, 1:2], rt[:, 3, 0:1]))
            link(V.tensor_scalar(rt[:, 11, 0:2], rt[:, 2, 0:2], rt[:, 3, 1:2], None, ALU.mult))
            link(V.tensor_reduce(rt[:, 12, 0:1], rt[:, 11, 0:2], AX.X, ALU.add))
            link(V.tensor_scalar(rt[:, 12, 1:2], rt[:, 12, 0:1], GATE_EPS, None, ALU.max))
            link(V.reciprocal(rt[:, 12, 2:3], rt[:, 12, 1:2]))
            link(V.tensor_scalar(rt[:, 13, 0:2], rt[:, 11, 0:2], rt[:, 12, 2:3], None, ALU.mult))
            dve.wait_ge(xd_psum, 1)
            V.tensor_copy(xd[:, 0], ps[:, 3]).then_inc(xd_ready, 1)
            dve.wait_ge(oh_ready, 1)
            link(V.tensor_scalar(gated[:], slot_no, slot[0], rt[:, 13, 0:1], ALU.is_equal, ALU.mult))
            dve.wait_ge(xd_psum, 2)
            link(V.tensor_scalar(onehot[:], slot_no, slot[1], rt[:, 13, 1:2], ALU.is_equal, ALU.mult))
            V.tensor_tensor(gated[:], gated[:], onehot[:], ALU.add).then_inc(gated_ready, 1)
            dve.wait_ge(zero_ready, 4)

            def bias_and_silu(n):
                for half in range(2):
                    chunks = slice(4 * half, 4 * half + 4)
                    dve.wait_ge(hidT_psum, 2 * n + half + 1)
                    if n >= 1:
                        dve.wait_ge(hT_ready, 2 * (n - 1) + half + 1)
                    bias = b1[:, 2 * n:2 * n + 2, chunks].rearrange("p e c -> p c e").unsqueeze(3)
                    V.tensor_tensor(hu[:, chunks],
                                    ps[:, 6 + half].rearrange("p (c e s) -> p c e s", c=4, e=2)[:, :, :, 0:CAP],
                                    bias.broadcast_to([P, 4, 2, CAP]), ALU.add).then_inc(hu_ready, 1)
                for half in range(2):
                    chunks = slice(4 * half, 4 * half + 4)
                    dve.wait_ge(ht_ready, 2 * n + half + 1)
                    if n >= 2:
                        dve.wait_ge(y_psum, n - 1)
                    V.scalar_tensor_tensor(out=hT[:, n % 2, chunks, :, 0:CAP], in0=ht[:, chunks], scalar=1.0,
                                           in1=hu[:, chunks], op0=ALU.add, op1=ALU.mult).then_inc(hT_ready, 1)

            def rows_out(n):
                dve.wait_ge(y_psum, n + 1)
                if n >= 2:
                    dve.wait_ge(c_psum, n - 1)
                V.scalar_tensor_tensor(out=ysb[:, n % 2], in0=ps[:, 2, 0:D], scalar=0.5, in1=b2[:, n],
                                       op0=ALU.mult, op1=ALU.add).then_inc(y_ready, 1)

            bias_and_silu(0)
            for n in range(1, E // 2):
                if n < E // 2 - 1:
                    rows_out(n - 1)
                    bias_and_silu(n)
                else:
                    rows_out(n - 1)
                    bias_and_silu(n)
            rows_out(E // 2 - 1)
            dve.wait_ge(c_psum, E // 2)
            link(V.tensor_tensor(fin[:, 0], xn[:], ps[:, 4, 0:D], ALU.add))
            norm_stats(3, fin[:, 0])
            link(normalise(3, fin[:, 1], fin[:, 0]))
            link(V.tensor_tensor(fin[:, 0], fin[:, 1], gamma[:], ALU.mult))
            dve.wait_ge(x2_ready, 1)
            V.tensor_tensor(fin[:, 2], fin[:, 0], x2[:], ALU.add).then_inc(out_ready, 1)

        @block.tensor
        def _(pe):
            MM = nc.tensor.matmul

            def transpose_xn(n):
                pe.wait_ge(xn_ready, n + 1)
                for c in range(DC):
                    last = nc.tensor.transpose(ps[:, 0, c * P:(c + 1) * P], xn[:, c * P:(c + 1) * P], eye)
                last.then_inc(xnT_psum, 1)

            def split_product(dst, lhs, rhs, start, stop):
                parts = [(0, 0), (0, 1), (1, 0)]
                for m, (i, j) in enumerate(parts):
                    last = MM(dst, lhs[i], rhs[j], start=start and m == 0, stop=stop and m == len(parts) - 1)
                return last

            def project_keys(kp):
                u, j = divmod(kp, PG)
                b, c, g = units[u]
                n = b * NC + c
                pe.wait_ge(ctxT_ready, n + 1)
                pe.wait_ge(wk_ready, g + 1)
                if kp >= 2:
                    pe.wait_ge(k_ready, kp - 1)
                cols = slice((g * PG + j) * P, (g * PG + j + 1) * P)
                for d in range(DC):
                    last = split_product(ps[:, K_BANK + kp % 2], [w[:, d, cols] for w in (w_k_h, w_k_l)],
                                         [x[:, n % 2, d, :] for x in (ctxT_h, ctxT_l)], d == 0, d == DC - 1)
                last.then_inc(k_psum, 1)

            def scores(s):
                u, t = divmod(s, KT)
                b, c, g = units[u]
                pe.wait_ge(k_ready, PG * (u + 1))
                if s >= 2:
                    pe.wait_ge(e_ready, s - 1)
                for j in range(PG):
                    last = MM(ps[:, S_BANK + s % 2, j * P:(j + 1) * P],
                              keys[:, PG * (u % 2) + j, t * P:(t + 1) * P], q_blk[:, g * PG + j, b, :],
                              start=True, stop=True)
                last.then_inc(s_psum, 1)

            def weighted_sum(s):
                u, t = divmod(s, KT)
                b, c, g = units[u]
                n = b * NC + c
                pe.wait_ge(el_ready, s + 1)
                pe.wait_ge(ctx_ready, n + 1)
                if b == 1 and c == 0 and t == 0:
                    pe.wait_ge(mixT_ready, DC * (g + 1))
                for half in range(DC):
                    cols = slice(half * P, (half + 1) * P)
                    last = split_product(ps[:, mix_bank(half, g)], [x[:, n % 2, t, cols] for x in (ctx_h, ctx_l)],
                                         [x[:, s % NE, :] for x in (ex_h, ex_l)], c == 0 and t == 0,
                                         c == NC - 1 and t == KT - 1)
                last.then_inc(mix_done, 1)

            def denominators(g, bank):
                pe.wait_ge(esum_ready, STEPS - (G - 1 - g) * KT)
                heads = range(HG * g, HG * (g + 1))
                MM(ps[:, bank, 0:HG], null_ex[:], eye[0:H, HG * g:HG * (g + 1)], start=True, stop=False,
                   skip_group_check=True)
                for n, h in enumerate(heads):
                    last = MM(ps[:, bank, n:n + 1], ex_sum[:, h].rearrange("p b q -> p (b q)"), ones[:, 0:1],
                              start=False, stop=n == HG - 1, skip_group_check=True)
                last.then_inc(den_psum, 1)

            def null_values(g):
                MM(ps[:, K_BANK + g], null_ex[:], null_v[:, 512 * g:512 * (g + 1)], start=True, stop=False,
                   skip_group_check=True)

            def values(g):
                pe.wait_ge(mixT_ready, DC * (G + g + 1))
                pe.wait_ge(ld_wv, 32)
                for n, h in enumerate(range(HG * g, HG * (g + 1))):
                    for half in range(DC):
                        last = MM(ps[:, K_BANK + g, n * DH:(n + 1) * DH],
                                  mixT[:, half, h].rearrange("p b q -> p (b q)"), w_v[:, half, h * DH:(h + 1) * DH],
                                  start=False, stop=n == HG - 1 and half == DC - 1, skip_group_check=True)
                last.then_inc(o_psum, 1)

            def transpose_mixed(g):
                pe.wait_ge(o_ready, g + 1)
                if g:
                    pe.wait_ge(oT_ready, g)
                for n in range(4):
                    last = nc.tensor.transpose(ps[:, 0, n * P:(n + 1) * P],
                                               mixed[:, 512 * g + n * P:512 * g + (n + 1) * P], eye)
                last.then_inc(oT_psum, 1)

            def output(g):
                pe.wait_ge(oT_ready, g + 1)
                for n in range(4 * g, 4 * g + 4):
                    last = MM(ps[:, 1, 0:D], mixedT[:, n], w_out[:, n], start=n == 0, stop=n == FC - 1)
                if g == G - 1:
                    last.then_inc(wo_psum, 1)

            pe.wait_ge(ld_const, 16)
            transpose_xn(0)
            project_keys(0)
            project_keys(1)
            pe.wait_ge(xnT_ready, 1)
            pe.wait_ge(ld_wq, 16)
            for j in range(NPAIR):
                for c in range(DC):
                    last = MM(ps[:, 1 + j // 4, (j % 4) * P:(j % 4 + 1) * P], w_q[:, c, j * P:(j + 1) * P],
                              xnT[:, c], start=c == 0, stop=c == DC - 1)
                if j % 4 == 3:
                    last.then_inc(q_psum, 1)
            project_keys(2)
            project_keys(3)
            pe.wait_ge(q_tanh, 2)
            pe.wait_ge(nk_tanh, 1)
            for j in range(NPAIR):
                last = MM(ps[0:H, 3, 0:P], null_kt[:, j], qT[:, j], start=j == 0, stop=j == NPAIR - 1)
            last.then_inc(null_psum, 1)
            pe.wait_ge(q_ready, 4)
            LAG = 2
            for s in range(STEPS + LAG):
                if s == LAG:
                    pe.wait_ge(null_ready, 1)
                if s < STEPS:
                    scores(s)
                    if s + KT < STEPS:
                        project_keys(s + KT)
                if s >= LAG:
                    weighted_sum(s - LAG)
            pe.wait_ge(k_ready, STEPS)
            denominators(0, 5)
            null_values(0)
            values(0)
            transpose_mixed(0)
            pe.wait_ge(o_ready, 1)
            denominators(1, 6)
            null_values(1)
            values(1)
            output(0)
            transpose_mixed(1)
            output(1)

            transpose_xn(1)
            pe.wait_ge(xnT_ready, 2)
            pe.wait_ge(ld_lin, 16 * 8)
            for c in range(DC):
                last = MM(ps[0:LR, 2, 0:P], w_gk1[:, c], xnT[:, c], start=c == 0, stop=c == DC - 1)
            last.then_inc(low_psum, 1)
            for w, weight in enumerate((w_lq, w_lk)):
                for j in range(2):
                    for c in range(DC):
                        last = MM(ps[:, 1, (2 * w + j) * P:(2 * w + j + 1) * P], weight[:, c, j * P:(j + 1) * P],
                                  xnT[:, c], start=c == 0, stop=c == DC - 1)
            last.then_inc(qk_psum, 1)
            pe.wait_ge(low_ready, 1)
            MM(ps[:, 3, 0:LH * LDK], lowT[0:LR + 1], w_gk2[0:LR + 1], start=True, stop=True).then_inc(logit_psum, 1)
            for c in range(DC):
                last = MM(ps[:, 4], xnT[:, c], w_lv[:, c], start=c == 0, stop=c == DC - 1)
            last.then_inc(v_psum, 1)
            for c in range(DC):
                last = MM(ps[:, 5], xnT[:, c], w_lg[:, c], start=c == 0, stop=c == DC - 1)
            last.then_inc(g_psum, 1)
            pe.wait_ge(g_ready, 1)
            for pair in range(2):
                bank = (6, 2)[pair]
                lhs = gate[:, 3, pair * P:(pair + 1) * P]
                MM(ps[:, bank], lhs, const[:, C_DECAY:C_DECAY + 512], start=True, stop=True)
                MM(ps[:, bank + 1, 0:NL * P - 512], lhs, const[:, C_DECAY + 512:C_DECAY + NL * P], start=True,
                   stop=True).then_inc(dec_psum, 1)
            pe.wait_ge(qk_ready, 3)
            for h in range(LH):
                last = MM(ps[:, 0, h * P:(h + 1) * P], lkT[:, h // 2], lqT[:, h // 2, h % 2], start=True, stop=True)
            last.then_inc(lev_psum, 1)
            pe.wait_ge(kx_ready, 2)
            pe.wait_ge(dec_ready, 2)
            for n in range(NL):
                pe.wait_ge(qx_ready, NL + n + 1)
                for h in range(LH):
                    at = 256 * (n % 2) + 64 * h
                    last = MM(ps[:, (1, 6, 7)[n // 2], at:at + 64], kx[:, h // 2, n], qx[:, h // 2, h % 2, n],
                              start=True, stop=True)
                if n % 2:
                    last.then_inc(lev_psum, 1)
            pe.wait_ge(att_ready, 1)
            pe.wait_ge(v_ready, 1)
            for h in range(LH):
                last = MM(ps[:, 2, h * LDV:(h + 1) * LDV], att[:, h], lv[:, h * LDV:(h + 1) * LDV], start=True,
                          stop=True)
            last.then_inc(lo_psum, 1)
            pe.wait_ge(lo_ready, 1)
            for h in range(LH):
                last = nc.tensor.transpose(ps[:, 3, h * P:(h + 1) * P], lo[:, 0, h * P:(h + 1) * P], eye)
            last.then_inc(loT_psum, 1)
            pe.wait_ge(loT_ready, 1)
            for h in range(LH):
                last = MM(ps[:, 4, 0:D], loT[:, h], w_lo[:, h], start=h == 0, stop=h == LH - 1)
            last.then_inc(lw_psum, 1)

            transpose_xn(2)
            pe.wait_ge(xnT_ready, 3)
            for c in range(DC):
                last = MM(ps[:, 1, 0:E], xnT[:, c], w_route[:, c], start=c == 0, stop=c == DC - 1)
            last.then_inc(rl_psum, 1)
            pe.wait_ge(pick_ready, 2)
            MM(ps[:, 2, 0:2 * E], strict, pick[:].rearrange("p k e -> p (k e)"), start=True, stop=False,
               skip_group_check=True)
            MM(ps[:, 2, E:2 * E], ones, pick[:, 0], start=False, stop=True, skip_group_check=True).then_inc(loc_psum, 1)
            pe.wait_ge(oh_ready, 1)
            for c in range(DC):
                MM(ps[:, (3, 5)[c]], xn[:, c * P:(c + 1) * P], onehot[:], start=True, stop=True).then_inc(xd_psum, 1)
            pe.wait_ge(xd_ready, 2)

            def up(n):
                for j in range(2):
                    pe.wait_ge(ld_exp[2 * n + j], 32)
                for half in range(2):
                    if n:
                        pe.wait_ge(hid_ready, 2 * (n - 1) + half + 1)
                    for c in range(DC):
                        for j in range(2):
                            e = 2 * n + j
                            last = MM(ps[SLOTS * j:SLOTS * (j + 1), half], xd[:, c, e * SLOTS:(e + 1) * SLOTS],
                                      w1[e][:, c, half * 512:(half + 1) * 512], start=c == 0, stop=c == DC - 1)
                    last.then_inc(f1_psum, 1)

            def turn(n):
                for half in range(2):
                    pe.wait_ge(hid_ready, 2 * n + half + 1)
                    if n:
                        pe.wait_ge(hu_ready, 2 * (n - 1) + half + 1)
                    for c in range(4):
                        last = nc.tensor.transpose(ps[:, 6 + half, c * P:(c + 1) * P],
                                                   hid[:, (4 * half + c) * P:(4 * half + c + 1) * P], eye)
                    last.then_inc(hidT_psum, 1)

            def down(n):
                pe.wait_ge(hT_ready, 2 * n + 2)
                if n:
                    pe.wait_ge(y_ready, n)
                for c in range(FC):
                    for j in range(2):
                        last = MM(ps[SLOTS * j:SLOTS * (j + 1), 2, 0:D], hT[:, n % 2, c, j], w2[2 * n + j][:, c],
                                  start=c == 0, stop=c == FC - 1)
                last.then_inc(y_psum, 1)

            def combine(n):
                pe.wait_ge(y_ready, n + 1)
                if n == 0:
                    pe.wait_ge(gatedT_ready, 1)
                MM(ps[:, 4, 0:D], gatedT[:, n], ysb[:, n % 2], start=n == 0, stop=n == E // 2 - 1).then_inc(c_psum, 1)

            up(0)
            turn(0)
            pe.wait_ge(gated_ready, 1)
            for n in range(E // 2):
                last = nc.tensor.transpose(ps[:, 3, n * P:(n + 1) * P], gated[:, n * P:(n + 1) * P], eye)
            last.then_inc(gatedT_psum, 1)
            up(1)
            down(0)
            turn(1)
            up(2)
            combine(0)
            down(1)
            turn(2)
            up(3)
            turn(3)
            combine(1)
            down(2)
            combine(2)
            down(3)
            combine(3)


_PLAIN = {
    "Wq": "L0_xattn_Wq", "Wkv": "L0_xattn_Wkv", "Wout": "L0_xattn_Wout", "bout": "L0_xattn_bout",
    "lWq": "L0_attn_Wq", "lWk": "L0_attn_Wk", "lWv": "L0_attn_Wv", "lWg": "L0_attn_Wg", "lWo": "L0_attn_Wo",
    "Wgk1": "L0_attn_Wgk1", "gnorm": "L0_attn_g_norm_weight", "wg": "L0_ffn_wg", "fc2": "L0_ffn_fc2_w",
    "b2": "L0_ffn_fc2_b", "gamma": "L0_ffn_ln_gamma", "beta": "L0_ffn_ln_beta",
}


def kernel(**inputs):
    import concourse.bacc as _bacc
    from concourse.bass_utils import run_bass_kernel_spmd as _run

    v = {k: np.ascontiguousarray(x) for k, x in inputs.items()}
    arrays = {short: v[name] for short, name in _PLAIN.items()}
    arrays["x"] = v["x"].reshape(P, D)
    arrays["ctx"] = v["ctx_1024"].reshape(B * NK, D)
    arrays["ctxT"] = arrays["ctx"].T
    arrays["Wgk2b"] = np.concatenate([v["L0_attn_Wgk2"], v["L0_attn_bgk2"][None, :]])
    arrays["fc1T"] = v["L0_ffn_fc1_w"].transpose(0, 2, 1)
    arrays["b1"] = v["L0_ffn_fc1_b"].reshape(E, FC, P).transpose(2, 0, 1)
    null_k = np.zeros((P, NPAIR, H), np.float32)
    null_v = np.zeros((H, INNER), np.float32)
    for h in range(H):
        rows = slice(DH * (h % 2), DH * (h % 2) + DH)
        null_k[rows, h // 2, h] = v["L0_xattn_null_key"]
        null_v[h, h * DH:(h + 1) * DH] = v["L0_xattn_null_value"]
    arrays["null_k"], arrays["null_v"] = null_k, null_v
    arrays["const"] = shape_constants()

    nc = _bacc.Bacc("TRN2", target_bir_lowering=False, num_devices=1)
    feed, a = {}, {}
    for name, x in arrays.items():
        feed[f"in_{name}"] = x = np.ascontiguousarray(x)
        a[name] = nc.dram_tensor(f"in_{name}", x.shape, mybir.dt.from_np(x.dtype), kind="ExternalInput").ap()
    out = nc.dram_tensor("out_x", (P, D), F32, kind="ExternalOutput").ap()
    block_kernel(nc, a, out)
    r = _run(nc, [feed], core_ids=[0])
    return r.results[0]["out_x"].reshape(B, S, D)
```

```python
from contextlib import ExitStack

import numpy as np

import concourse.bass as bass
from concourse import mybir

F32 = mybir.dt.float32
F32R = mybir.dt.float32r
U32 = mybir.dt.uint32
ALU = mybir.AluOpType
ACT = mybir.ActivationFunctionType
AX = mybir.AxisListType

P = 128
B, S, D = 2, 64, 256
NK = 1024
H, DH = 16, 64
INNER = H * DH
DC = D // P
CK = 256
NC = NK // CK
KT = CK // P
G = 2
HG = H // G
PG = HG // 2
NPAIR = H // 2
PK = PG // KT
LH, LDK, LDV, LR = 4, 64, 128, 16
LEVELS = [32, 16, 8, 4, 2, 1]
NL = len(LEVELS)
GATE_NORM = 16.0
E, FH = 8, 1024
FC = FH // P
N_TOK = B * S
CAP = 2 * int(1.25 * ((N_TOK + E - 1) // E))
SLOTS = 64
LN_EPS = 1e-5
GATE_EPS = 1.1920929e-07
assert B * S == P and CAP <= SLOTS

C_EYE, C_ONES, C_STRICT, C_IOTA8, C_MASK, C_DECAY, C_SLOT = 0, 128, 256, 384, 392, 776, 1544
C_WIDTH = C_SLOT + E * SLOTS


def shape_constants():
    c = np.zeros((P, C_WIDTH), np.float32)
    t = np.arange(P)
    c[:, C_EYE:C_EYE + P] = np.eye(P)
    c[:, C_STRICT:C_STRICT + P] = t[:, None] < t[None, :]
    c[:, C_ONES:C_ONES + P] = 1.0
    c[:, C_IOTA8:C_IOTA8 + E] = np.arange(E)
    for n, half in enumerate(LEVELS):
        block, right = t // (2 * half), t // half % 2 == 1
        edge = block * 2 * half + half
        cols = t[right]
        same = block[:, None] == block[None, cols]
        c[:, C_MASK + n * 64:C_MASK + (n + 1) * 64] = same & ~right[:, None]
        u, at = t[:, None], t[None, :]
        in_right = (u >= edge[None, :]) & (u <= at)
        in_left = (u > at) & (u < edge[None, :])
        c[:, C_DECAY + n * P:C_DECAY + (n + 1) * P] = np.where(right[None, :], in_right, in_left)
    c[:, C_SLOT:] = np.arange(1, E * SLOTS + 1)
    return c


def block_kernel(nc, a, out):
    with ExitStack() as whole:
        def sem(name):
            return whole.enter_context(nc.semaphore(name))

        def alloc(stack, name, shape, dt=F32):
            return stack.enter_context(nc.sbuf_tensor(name, shape, dt))

        ps = whole.enter_context(nc.psum_tensor("ps", [P, 8, 512], F32))

        def keep(name, shape, dt=F32):
            return alloc(whole, name, shape, dt)

        const = keep("const", [P, C_WIDTH])
        eye = const[:, C_EYE:C_EYE + P]
        strict = const[:, C_STRICT:C_STRICT + P]
        ones = const[:, C_ONES:C_ONES + P]
        iota8 = const[:, C_IOTA8:C_IOTA8 + E]
        slot_no = const[:, C_SLOT:C_SLOT + E * SLOTS]
        minus_half = keep("minus_half", [P, LH])
        x0 = keep("x0", [P, D])
        x1 = keep("x1", [P, D])
        x2 = keep("x2", [P, D])
        xn = keep("xn", [P, D])
        xnT = keep("xnT", [P, DC, P])
        bout = keep("bout", [P, D])
        gamma = keep("gamma", [P, D])
        beta = keep("beta", [P, D])
        gnorm = keep("gnorm", [P, LDV])
        stat = keep("stat", [P, 4, 16])
        w_lq = keep("w_lq", [P, DC, LH * LDK])
        w_lk = keep("w_lk", [P, DC, LH * LDK])
        w_lv = keep("w_lv", [P, DC, LH * LDV])
        w_lg = keep("w_lg", [P, DC, LH * LDV])
        w_lo = keep("w_lo", [P, LH, D])
        w_gk1 = keep("w_gk1", [P, DC, LR])
        w_gk2 = keep("w_gk2", [32, LH * LDK])
        w_route = keep("w_route", [P, DC, E])
        b1 = keep("b1", [P, E, FC])
        b2 = keep("b2", [P, E // 2, D])

        attn_a = ExitStack()
        w_k_stage = alloc(attn_a, "w_k_stage", [P, G, DC, INNER // G])
        stage_t = alloc(attn_a, "stage_t", [P, 2, DC, CK])
        stage_n = alloc(attn_a, "stage_n", [P, 2, KT, D])
        w_k_h = alloc(attn_a, "w_k_h", [P, G, DC, INNER // G], F32R)
        w_k_l = alloc(attn_a, "w_k_l", [P, G, DC, INNER // G], F32R)
        ctxT_h = alloc(attn_a, "ctxT_h", [P, 2, DC, CK], F32R)
        ctxT_l = alloc(attn_a, "ctxT_l", [P, 2, DC, CK], F32R)
        keys = alloc(attn_a, "keys", [P, 2, PG, CK])
        ctx_h = alloc(attn_a, "ctx_h", [P, 2, KT, D], F32R)
        ctx_l = alloc(attn_a, "ctx_l", [P, 2, KT, D], F32R)
        NE = 4
        ex = alloc(attn_a, "ex", [P, NE, 512])
        ex_h = alloc(attn_a, "ex_h", [P, NE, 512], F32R)
        ex_l = alloc(attn_a, "ex_l", [P, NE, 512], F32R)
        q_blk = alloc(attn_a, "q_blk", [P, NPAIR, B, P])
        alloc(attn_a, "unused", [P, 6144])
        attn_b = ExitStack()
        w_v = alloc(attn_b, "w_v", [P, DC, INNER])
        w_out = alloc(attn_b, "w_out", [P, FC, D])
        mixT = alloc(attn_b, "mixT", [P, DC, H, B, S])
        ex_sum = alloc(attn_b, "ex_sum", [P, H, B, S])
        w_q = mixT[:, 0].rearrange("p h b s -> p (h b s)").rearrange("p (c n) -> p c n", c=DC)
        null_v = alloc(attn_b, "null_v", [P, INNER])
        null_k = alloc(attn_b, "null_k", [P, NPAIR, H])
        null_kt = alloc(attn_b, "null_kt", [P, NPAIR, H])
        null_ex = alloc(attn_b, "null_ex", [P, P])
        qT = alloc(attn_b, "qT", [P, NPAIR, P])
        mixedT = alloc(attn_b, "mixedT", [P, FC, P])
        share = alloc(attn_b, "share", [P, G, PG, P])
        attn_b.close()
        attn_a.close()

        w1, w2 = [], []
        for e in range(E):
            w1.append(keep(f"w1_{e}", [P, DC, FH]))
            w2.append(keep(f"w2_{e}", [P, FC, D]))

        lin = ExitStack()
        lqT = alloc(lin, "lqT", [P, 2, 2, P])
        lkT = alloc(lin, "lkT", [P, 2, P])
        lowT = alloc(lin, "lowT", [32, P])
        gate = alloc(lin, "gate", [P, 4, LH * LDK])
        lv = alloc(lin, "lv", [P, LH * LDV])
        silu = alloc(lin, "silu", [P, 2, LH * LDV])
        decay = alloc(lin, "decay", [P, 2, NL, P])
        kx = alloc(lin, "kx", [P, 2, NL, P])
        qx = alloc(lin, "qx", [P, 2, NL, 2, 64])
        att = alloc(lin, "att", [P, LH, P])
        lo = alloc(lin, "lo", [P, 3, LH * LDV])
        loT = alloc(lin, "loT", [P, LH, P])
        lstat = alloc(lin, "lstat", [P, 4, LH])
        lin.close()

        moe = whole
        rt = alloc(moe, "rt", [P, 16, 8])
        rt_idx = alloc(moe, "rt_idx", [P, 8], U32)
        pick = alloc(moe, "pick", [P, 2, E])
        onehot = alloc(moe, "onehot", [P, E * SLOTS])
        gated = alloc(moe, "gated", [P, E * SLOTS])
        gatedT = alloc(moe, "gatedT", [P, E // 2, P])
        xd = alloc(moe, "xd", [P, DC, E * SLOTS])
        hid = alloc(moe, "hid", [P, FH])
        hu = alloc(moe, "hu", [P, FC, 2, CAP])
        ht = alloc(moe, "ht", [P, FC, 2, CAP])
        hT = alloc(moe, "hT", [P, 2, FC, 2, SLOTS])
        ysb = alloc(moe, "ysb", [P, 2, D])
        fin = alloc(moe, "fin", [P, 3, D])

        ld_x = sem("ld_x")
        ld_eye = sem("ld_eye")
        ld_const = sem("ld_const")
        null_sums = sem("null_sums")
        half_ready = sem("half_ready")
        ld_wq = sem("ld_wq")
        ld_wk = [[sem(f"ld_wk{g}{d}") for d in range(DC)] for g in range(G)]
        ld_ctx = [sem(f"ld_ctx{n}") for n in range(B * NC)]
        ld_ctxT = [sem(f"ld_ctxT{n}") for n in range(B * NC)]
        ld_null = sem("ld_null")
        ld_null_v = sem("ld_null_v")
        ld_wv = sem("ld_wv")
        ld_lin = sem("ld_lin")
        ld_small = sem("ld_small")
        ld_exp = [sem(f"ld_exp{e}") for e in range(E)]
        st_out = sem("st_out")
        dve_seq = sem("dve_seq")
        act_seq = sem("act_seq")
        var_ready = sem("var_ready")
        rstd_ready = sem("rstd_ready")
        xn_ready = sem("xn_ready")
        xnT_psum = sem("xnT_psum")
        xnT_ready = sem("xnT_ready")
        zero_ready = sem("zero_ready")
        zero_ql = sem("zero_ql")
        q_psum = sem("q_psum")
        q_tanh = sem("q_tanh")
        q_ready = sem("q_ready")
        nk_tanh = sem("nk_tanh")
        null_psum = sem("null_psum")
        null_ready = sem("null_ready")
        wk_high = sem("wk_high")
        wk_ready = sem("wk_ready")
        ctxT_high = sem("ctxT_high")
        ctxT_ready = sem("ctxT_ready")
        ctx_ready = sem("ctx_ready")
        k_psum = sem("k_psum")
        k_ready = sem("k_ready")
        s_psum = sem("s_psum")
        e_ready = sem("e_ready")
        el_ready = sem("el_ready")
        esum_ready = sem("esum_ready")
        mix_done = sem("mix_done")
        mixT_ready = sem("mixT_ready")
        mixT_half = sem("mixT_half")
        den_psum = sem("den_psum")
        o_psum = sem("o_psum")
        o_ready = sem("o_ready")
        wo_psum = sem("wo_psum")
        x1_ready = sem("x1_ready")
        low_psum = sem("low_psum")
        low_ready = sem("low_ready")
        logit_psum = sem("logit_psum")
        qk_psum = sem("qk_psum")
        qk_ready = sem("qk_ready")
        v_psum = sem("v_psum")
        v_ready = sem("v_ready")
        g_psum = sem("g_psum")
        gln_ready = sem("gln_ready")
        g_ready = sem("g_ready")
        dec_psum = sem("dec_psum")
        dec_ready = sem("dec_ready")
        gtanh_ready = sem("gtanh_ready")
        kx_ready = sem("kx_ready")
        qx_ready = sem("qx_ready")
        lev_psum = sem("lev_psum")
        att_ready = sem("att_ready")
        lo_psum = sem("lo_psum")
        sq_ready = sem("sq_ready")
        ms_ready = sem("ms_ready")
        lr_ready = sem("lr_ready")
        lo_ready = sem("lo_ready")
        loT_psum = sem("loT_psum")
        loT_ready = sem("loT_ready")
        lw_psum = sem("lw_psum")
        x2_ready = sem("x2_ready")
        rl_psum = sem("rl_psum")
        rd_ready = sem("rd_ready")
        rexp_ready = sem("rexp_ready")
        pick_ready = sem("pick_ready")
        loc_psum = sem("loc_psum")
        oh_ready = sem("oh_ready")
        xd_psum = sem("xd_psum")
        xd_ready = sem("xd_ready")
        gated_ready = sem("gated_ready")
        gatedT_psum = sem("gatedT_psum")
        gatedT_ready = sem("gatedT_ready")
        f1_psum = sem("f1_psum")
        hid_ready = sem("hid_ready")
        hidT_psum = sem("hidT_psum")
        hu_ready = sem("hu_ready")
        ht_ready = sem("ht_ready")
        hT_ready = sem("hT_ready")
        y_psum = sem("y_psum")
        y_ready = sem("y_ready")
        c_psum = sem("c_psum")
        out_ready = sem("out_ready")

        units = [(b, c, g) for b in range(B) for c in range(NC) for g in range(G)]
        NU = len(units)
        STEPS = NU * KT
        AHEAD = KT + 1

        def mix_bank(half, g):
            return 2 * half + g
        K_BANK, S_BANK = 4, 6

        def den_bank(g):
            return (4, 6)[g]

        def value_bank(g):
            return (5, 7)[g]

        block = whole.enter_context(nc.Block())

        @block.sync
        def _(sp):
            def load_chunk(n):
                b, c = n // NC, n % NC
                if n >= 2:
                    sp.wait_ge(ctx_ready, n - 1)
                cols = slice(b * NK + c * CK, b * NK + (c + 1) * CK)
                sp.dma_start(stage_t[:, n % 2], a["ctxT"][:, cols].rearrange("(c p) n -> p c n", p=P)).then_inc(ld_ctxT[n], 16)
                if n:
                    sp.dma_start(stage_n[:, n % 2], a["ctx"][cols, :].rearrange("(t p) d -> p t d", p=P)).then_inc(ld_ctx[n], 16)

            def load_wk(g):
                for d in range(DC):
                    sp.dma_start(w_k_stage[:, g, d],
                                 a["Wkv"][d * P:(d + 1) * P, g * 512:(g + 1) * 512]).then_inc(ld_wk[g][d], 16)

            def chunked(name, p=P):
                return a[name].rearrange("(c p) n -> p c n", p=p)

            def rows(name, n=P):
                return a[name].rearrange("(o d) -> o d", o=1).broadcast_to([n, a[name].shape[0]])

            sp.dma_start(x0[:], a["x"]).then_inc(ld_x, 16)
            sp.dma_start(const[:, 0:C_STRICT], a["const"][:, 0:C_STRICT]).then_inc(ld_eye, 16)
            load_chunk(0)
            load_wk(0)
            sp.dma_start(w_q, chunked("Wq")).then_inc(ld_wq, 16)
            sp.dma_start(null_k[:], a["null_k"]).then_inc(ld_null, 16)
            sp.dma_start(stage_n[:, 0], a["ctx"][0:CK, :].rearrange("(t p) d -> p t d", p=P)).then_inc(ld_ctx[0], 16)
            load_wk(1)
            load_chunk(1)
            sp.wait_ge(zero_ready, 2)
            sp.dma_start(null_v[0:H], a["null_v"]).then_inc(ld_null_v, 16)
            sp.dma_start(const[:, C_STRICT:], a["const"][:, C_STRICT:]).then_inc(ld_const, 16)
            sp.dma_start(bout[:], rows("bout")).then_inc(ld_small, 16)
            sp.dma_start(gamma[:], rows("gamma")).then_inc(ld_small, 16)
            sp.dma_start(beta[:], rows("beta")).then_inc(ld_small, 16)
            sp.dma_start(gnorm[:], rows("gnorm")).then_inc(ld_small, 16)
            sp.dma_start(b1[:], a["b1"]).then_inc(ld_small, 16)
            for e in range(E):
                half = SLOTS * (e % 2)
                sp.dma_start(b2[half:half + SLOTS, e // 2, :],
                             a["b2"][e:e + 1, :].broadcast_to([SLOTS, D])).then_inc(ld_small, 16)
            sp.dma_start(w_v[:], a["Wkv"][:, INNER:2 * INNER].rearrange("(c p) n -> p c n", p=P)).then_inc(ld_wv, 16)
            sp.dma_start(w_out[:], chunked("Wout")).then_inc(ld_wv, 16)
            load_chunk(2)
            sp.dma_start(w_lq[:], chunked("lWq")).then_inc(ld_lin, 16)
            sp.dma_start(w_lk[:], chunked("lWk")).then_inc(ld_lin, 16)
            sp.dma_start(w_lv[:], chunked("lWv")).then_inc(ld_lin, 16)
            sp.dma_start(w_lg[:], chunked("lWg")).then_inc(ld_lin, 16)
            sp.dma_start(w_lo[:], chunked("lWo")).then_inc(ld_lin, 16)
            sp.dma_start(w_gk1[:], chunked("Wgk1")).then_inc(ld_lin, 16)
            sp.dma_start(w_gk2[0:LR + 1], a["Wgk2b"]).then_inc(ld_lin, 16)
            sp.dma_start(w_route[:], chunked("wg")).then_inc(ld_lin, 16)
            for n in range(3, B * NC):
                load_chunk(n)
            for e in range(E):
                if e == 0:
                    sp.wait_ge(ctx_ready, B * NC)
                if e == 1:
                    sp.wait_ge(k_psum, STEPS)
                if e == 2:
                    sp.wait_ge(mix_done, STEPS)
                    sp.wait_ge(esum_ready, STEPS)
                if e == 7:
                    sp.wait_ge(wo_psum, 1)
                sp.dma_start(w1[e][:], a["fc1T"][e].rearrange("(c p) n -> p c n", p=P)).then_inc(ld_exp[e], 16)
                sp.dma_start(w2[e][:], a["fc2"][e].rearrange("(c p) n -> p c n", p=P)).then_inc(ld_exp[e], 16)
            sp.wait_ge(out_ready, 1)
            sp.dma_start(out, fin[:, 2, :]).then_inc(st_out, 16)
            sp.wait_ge(st_out, 16)

        @block.gpsimd
        def _(pool):
            nc.gpsimd.memset(minus_half[:], -0.5).then_inc(half_ready, 1)
            pool.wait_ge(half_ready, 1)
            for n in range(3):
                pool.wait_ge(var_ready, n + 1)
                nc.gpsimd.tensor_tensor(stat[:, n, 9:10], stat[:, n, 8:9], minus_half[:, 0:1], ALU.pow).then_inc(rstd_ready, 1)
                if n == 0:
                    nc.gpsimd.memset(null_ex[:], 0.0).then_inc(zero_ready, 1)
                    nc.gpsimd.memset(null_v[:], 0.0).then_inc(zero_ready, 1)
                    nc.gpsimd.memset(ex_sum[:], 0.0).then_inc(zero_ready, 1)
                    pool.wait_ge(zero_ready, 3)
                    pool.wait_ge(null_ready, 1)
                    pool.wait_ge(ld_eye, 16)
                    nc.gpsimd.tensor_tensor(ex_sum[0:H].rearrange("p h b q -> p h (b q)"),
                                            null_ex[0:H].unsqueeze(1).broadcast_to([H, H, P]),
                                            eye[0:H, 0:H].unsqueeze(2).broadcast_to([H, H, P]),
                                            ALU.mult).then_inc(null_sums, 1)
                    pool.wait_ge(wo_psum, 1)
                    nc.gpsimd.memset(lowT[:], 1.0).then_inc(zero_ready, 1)
                    nc.gpsimd.memset(lqT[:], 0.0).then_inc(zero_ready, 1)
                if n == 1:
                    pool.wait_ge(ms_ready, 1)
                    nc.gpsimd.tensor_tensor(lstat[:, 2], lstat[:, 1], minus_half[:], ALU.pow).then_inc(lr_ready, 1)
                    pool.wait_ge(lw_psum, 1)
                    nc.gpsimd.memset(hT[:], 0.0).then_inc(zero_ready, 1)
            pool.wait_ge(var_ready, 4)
            nc.gpsimd.tensor_tensor(stat[:, 3, 9:10], stat[:, 3, 8:9], minus_half[:, 0:1], ALU.pow).then_inc(rstd_ready, 1)

        @block.scalar
        def _(act):
            seq = [0]

            def link(ins):
                seq[0] += 1
                ins.then_inc(act_seq, 1)
                act.wait_ge(act_seq, seq[0])

            def copy(dst, src, done):
                nc.scalar.activation(dst, src, ACT.Copy).then_inc(done, 1)

            def split_wk(g):
                for d in range(DC):
                    act.wait_ge(ld_wk[g][d], 16)
                    copy(w_k_h[:, g, d], w_k_stage[:, g, d], wk_high)

            def keys_tanh(kp):
                u, i = divmod(kp, KT)
                act.wait_ge(k_psum, kp + 1)
                if u >= 2:
                    act.wait_ge(s_psum, KT * (u - 1))
                src = ps[:, K_BANK + kp % 2].rearrange("p (j n) -> p j n", j=PK)
                nc.scalar.activation(keys[:, u % 2, PK * i:PK * (i + 1)], src, ACT.Tanh).then_inc(k_ready, 1)

            act.wait_ge(ld_ctxT[0], 16)
            copy(ctxT_h[:, 0], stage_t[:, 0], ctxT_high)
            split_wk(0)
            act.wait_ge(ld_null, 16)
            nc.scalar.activation(null_kt[:], null_k[:], ACT.Tanh).then_inc(nk_tanh, 1)
            keys_tanh(0)
            for j in range(2):
                act.wait_ge(q_psum, j + 1)
                src = ps[:, 1 + j].rearrange("p (j t) -> p j t", t=P)
                nc.scalar.activation(qT[:, 4 * j:4 * j + 4], src, ACT.Tanh).then_inc(q_tanh, 1)
            split_wk(1)
            keys_tanh(1)
            keys_tanh(2)
            act.wait_ge(zero_ready, 1)
            act.wait_ge(null_psum, 1)
            nc.scalar.activation(null_ex[0:H], ps[0:H, 3, 0:P], ACT.Exp, scale=DH ** -0.5).then_inc(null_ready, 1)

            for s in range(STEPS):
                act.wait_ge(s_psum, s + 1)
                r = s % NE
                if s >= NE:
                    act.wait_ge(esum_ready, s - NE + 1)
                    act.wait_ge(mix_done, s - NE + 1)
                nc.scalar.activation(ex[:, r], ps[:, S_BANK + s % 2], ACT.Exp, scale=DH ** -0.5)
                nc.scalar.activation(ex_h[:, r], ps[:, S_BANK + s % 2], ACT.Exp, scale=DH ** -0.5).then_inc(e_ready, 1)
                if s + AHEAD < STEPS:
                    keys_tanh(s + AHEAD)
            act.preload_act_table_set("natural_log_exp_and_others")
            for g in range(G):
                act.wait_ge(mix_done, STEPS - (G - 1 - g) * KT)
                copy(mixT[:, 1, HG * g:HG * (g + 1), B - 1, :],
                     ps[:, mix_bank(1, g)].rearrange("p (h q) -> p h q", q=S), mixT_half)

            act.wait_ge(xnT_psum, 2)
            copy(xnT[:], ps[:, 0, 0:DC * P].rearrange("p (c t) -> p c t", c=DC), xnT_ready)
            act.wait_ge(logit_psum, 1)
            link(nc.scalar.activation(gate[:, 0], ps[:, 3, 0:D], ACT.Abs))
            link(nc.scalar.activation(gate[:, 1], gate[:, 0], ACT.Exp, scale=-1.0))
            nc.scalar.activation(gate[:, 2], gate[:, 1], ACT.Ln, bias=1.0).then_inc(gln_ready, 1)
            act.preload_act_table_set("exp_and_others")
            act.wait_ge(v_psum, 1)
            copy(lv[:], ps[:, 4], v_ready)
            for pair in range(2):
                act.wait_ge(dec_psum, pair + 1)
                bank = (6, 2)[pair]
                src = ps[:, bank:bank + 2, :].rearrange("p a n -> p (a n)")[:, 0:NL * P]
                nc.scalar.activation(decay[:, pair].rearrange("p l t -> p (l t)"), src, ACT.Exp,
                                     scale=1.0 / GATE_NORM).then_inc(dec_ready, 1)
            act.wait_ge(g_psum, 1)
            nc.scalar.activation(silu[:, 0], ps[:, 5], ACT.Tanh, scale=0.5).then_inc(gtanh_ready, 1)
            act.wait_ge(lo_psum, 1)
            nc.scalar.activation(lo[:, 0], ps[:, 2], ACT.Square).then_inc(sq_ready, 1)
            act.wait_ge(loT_psum, 1)
            copy(loT[:], ps[:, 3].rearrange("p (c t) -> p c t", t=P), loT_ready)

            act.wait_ge(xnT_psum, 3)
            copy(xnT[:], ps[:, 0, 0:DC * P].rearrange("p (c t) -> p c t", c=DC), xnT_ready)
            act.wait_ge(rd_ready, 1)
            nc.scalar.activation(rt[:, 2], rt[:, 1], ACT.Exp, accum_out=rt[:, 3, 0:1]).then_inc(rexp_ready, 1)
            act.wait_ge(xd_psum, 2)
            copy(xd[:, 1], ps[:, 5], xd_ready)
            for n in range(E // 2):
                for half in range(2):
                    act.wait_ge(f1_psum, 2 * n + half + 1)
                    if n >= 1:
                        act.wait_ge(hidT_psum, 2 * (n - 1) + half + 1)
                    copy(hid[:, half * 512:(half + 1) * 512], ps[:, half], hid_ready)
                for half in range(2):
                    act.wait_ge(hu_ready, 2 * n + half + 1)
                    if n >= 1:
                        act.wait_ge(hT_ready, 2 * (n - 1) + half + 1)
                    nc.scalar.activation(ht[:, 4 * half:4 * half + 4], hu[:, 4 * half:4 * half + 4], ACT.Tanh,
                                         scale=0.5).then_inc(ht_ready, 1)
                if n == 0:
                    act.wait_ge(gatedT_psum, 1)
                    copy(gatedT[:], ps[:, 3].rearrange("p (n t) -> p n t", t=P), gatedT_ready)

        @block.vector
        def _(dve):
            V = nc.vector
            seq = [0]

            def link(ins):
                seq[0] += 1
                ins.then_inc(dve_seq, 1)
                dve.wait_ge(dve_seq, seq[0])

            def norm_stats(n, src):
                link(V.bn_stats(stat[:, n, 0:6], src))
                link(V.bn_aggr(stat[:, n, 6:8], stat[:, n, 0:6]))
                V.tensor_scalar(stat[:, n, 8:9], stat[:, n, 7:8], LN_EPS, None, ALU.add).then_inc(var_ready, 1)

            def normalise(n, dst, src):
                dve.wait_ge(rstd_ready, n + 1)
                return V.tensor_scalar(dst, src, stat[:, n, 6:7], stat[:, n, 9:10], ALU.subtract, ALU.mult)

            def low_part(dst, full, high):
                return V.tensor_tensor(dst, full, high.bitcast(F32), ALU.subtract)

            def split_wk(g):
                for d in range(DC):
                    dve.wait_ge(wk_high, DC * g + d + 1)
                    low_part(w_k_l[:, g, d], w_k_stage[:, g, d], w_k_h[:, g, d]).then_inc(wk_ready, 1)

            def split_ctxT(n):
                r = n % 2
                if n == 0:
                    dve.wait_ge(ctxT_high, 1)
                else:
                    dve.wait_ge(ld_ctxT[n], 16)
                    if n >= 2:
                        dve.wait_ge(k_psum, G * KT * (n - 1))
                    link(V.tensor_copy(ctxT_h[:, r], stage_t[:, r]))
                low_part(ctxT_l[:, r], stage_t[:, r], ctxT_h[:, r]).then_inc(ctxT_ready, 1)

            def split_ctx(n):
                r = n % 2
                dve.wait_ge(ld_ctx[n], 16)
                if n >= 2:
                    dve.wait_ge(mix_done, G * KT * (n - 1))
                link(V.tensor_copy(ctx_h[:, r], stage_n[:, r]))
                low_part(ctx_l[:, r], stage_n[:, r], ctx_h[:, r]).then_inc(ctx_ready, 1)

            def evacuate(u, halves=DC):
                b, c, g = units[u]
                dve.wait_ge(mix_done, KT * (u + 1))
                for half in range(halves):
                    V.tensor_copy(mixT[:, half, HG * g:HG * (g + 1), b, :],
                                  ps[:, mix_bank(half, g)].rearrange("p (h q) -> p h q", q=S)).then_inc(mixT_ready, 1)

            V.memset(q_blk[:], 0.0).then_inc(zero_ql, 1)
            dve.wait_ge(ld_x, 16)
            norm_stats(0, x0[:])
            normalise(0, xn[:], x0[:]).then_inc(xn_ready, 1)
            split_ctxT(0)
            split_wk(0)
            dve.wait_ge(xnT_psum, 1)
            V.tensor_copy(xnT[:], ps[:, 0, 0:DC * P].rearrange("p (c t) -> p c t", c=DC)).then_inc(xnT_ready, 1)
            dve.wait_ge(zero_ql, 1)
            for j in range(2):
                for r in range(2):
                    rows, cols = slice(64 * r, 64 * r + 64), slice(S * r, S * r + S)
                    dve.wait_ge(q_tanh, j + 1)
                    V.tensor_copy(q_blk[rows, 4 * j:4 * j + 4, :, cols],
                                  qT[rows, 4 * j:4 * j + 4].rearrange("p j (b q) -> p j b q", b=B)).then_inc(q_ready, 1)
                if j == 0:
                    split_wk(1)
            split_ctx(0)

            for s in range(STEPS):
                u, t = divmod(s, KT)
                b, c, g = units[u]
                r = s % NE
                dve.wait_ge(e_ready, s + 1)
                if s >= NE:
                    dve.wait_ge(mix_done, s - NE + 1)
                low_part(ex_l[:, r], ex[:, r], ex_h[:, r]).then_inc(el_ready, 1)
                total = ex_sum[:, HG * g:HG * (g + 1), b, :]
                tile = ex[:, r].rearrange("p (h q) -> p h q", q=S)
                if s == 0:
                    dve.wait_ge(null_sums, 1)
                else:
                    dve.wait_ge(esum_ready, s)
                V.tensor_tensor(total, total, tile, ALU.add).then_inc(esum_ready, 1)
                n = b * NC + c
                if t == 0 and n + 1 < B * NC:
                    if g == 0:
                        split_ctxT(n + 1)
                    else:
                        split_ctx(n + 1)
                if t == 0 and u >= 2 and units[u - 2][1] == NC - 1:
                    evacuate(u - 2)

            def finish_group(g):
                dve.wait_ge(den_psum, g + 1)
                link(V.reciprocal(share[:, g], ps[:, den_bank(g)].rearrange("p (j t) -> p j t", t=P)))
                dve.wait_ge(o_psum, g + 1)
                V.tensor_tensor(mixedT[:, PG * g:PG * (g + 1)], ps[:, value_bank(g)].rearrange("p (j t) -> p j t", t=P),
                                share[:, g], ALU.mult).then_inc(o_ready, 1)

            evacuate(NU - 2, 1)
            finish_group(0)
            evacuate(NU - 1, 1)
            dve.wait_ge(ld_small, 16 * (5 + E))
            V.tensor_tensor(x1[:], x0[:], bout[:], ALU.add).then_inc(x1_ready, 1)
            finish_group(1)
            dve.wait_ge(wo_psum, 1)
            dve.wait_ge(x1_ready, 1)
            link(V.tensor_tensor(x1[:], x1[:], ps[:, 2, 0:D], ALU.add))

            norm_stats(1, x1[:])
            normalise(1, xn[:], x1[:]).then_inc(xn_ready, 1)
            dve.wait_ge(low_psum, 1)
            dve.wait_ge(zero_ready, 5)
            V.tensor_copy(lowT[0:LR], ps[0:LR, 2, 0:P]).then_inc(low_ready, 1)
            dve.wait_ge(qk_psum, 1)
            qk = ps[:, 1].rearrange("p (w j t) -> p w j t", w=2, j=2)
            for r in range(2):
                rows = slice(64 * r, 64 * r + 64)
                V.tensor_scalar(lqT[rows, :, r, :], qk[rows, 0], LDK ** -0.5, None, ALU.mult).then_inc(qk_ready, 1)
            V.tensor_copy(lkT[:], qk[:, 1]).then_inc(qk_ready, 1)
            dve.wait_ge(gln_ready, 1)
            V.scalar_tensor_tensor(out=gate[:, 3], in0=ps[:, 3, 0:D], scalar=0.0, in1=gate[:, 2], op0=ALU.min,
                                   op1=ALU.subtract).then_inc(g_ready, 1)
            dve.wait_ge(qk_ready, 3)
            for pair in range(2):
                dve.wait_ge(dec_ready, pair + 1)
                V.tensor_tensor(kx[:, pair], decay[:, pair],
                                lkT[:, pair].unsqueeze(1).broadcast_to([P, NL, P]), ALU.mult).then_inc(kx_ready, 1)
                for n, half in enumerate(LEVELS):
                    right = lqT[:, pair].rearrange("p r (m w l) -> p r m w l", w=2, l=half)[:, :, :, 1, :]
                    dec = decay[:, pair, n].rearrange("p (m w l) -> p m w l", w=2, l=half)[:, :, 1, :]
                    dec = dec.unsqueeze(1).broadcast_to([P, 2, 64 // half, half])
                    V.tensor_tensor(qx[:, pair, n].rearrange("p r (m l) -> p r m l", l=half), right, dec,
                                    ALU.mult).then_inc(qx_ready, 1)
            dve.wait_ge(ld_const, 16)
            dve.wait_ge(lev_psum, 1)
            link(V.tensor_tensor(att[:], ps[:, 0].rearrange("p (h t) -> p h t", t=P),
                                 eye.unsqueeze(1).broadcast_to([P, LH, P]), ALU.mult))
            for n, half in enumerate(LEVELS):
                dve.wait_ge(lev_psum, 2 + n // 2)
                src = ps[:, (1, 6, 7)[n // 2], 256 * (n % 2):256 * (n % 2) + 256].rearrange("p (h m l) -> p h m l", h=LH, l=half)
                mask = const[:, C_MASK + 64 * n:C_MASK + 64 * n + 64].bitcast(U32).rearrange("p (m l) -> p m l", l=half)
                mask = mask.unsqueeze(1).broadcast_to([P, LH, 64 // half, half])
                dst = att[:].rearrange("p h (m w l) -> p h m w l", w=2, l=half)[:, :, :, 1, :]
                ins = V.copy_predicated(dst, mask, src)
                if n + 1 < NL:
                    link(ins)
                else:
                    ins.then_inc(att_ready, 1)
            dve.wait_ge(gtanh_ready, 1)
            link(V.scalar_tensor_tensor(out=silu[:, 1], in0=silu[:, 0], scalar=1.0, in1=ps[:, 5], op0=ALU.add,
                                        op1=ALU.mult))
            V.scalar_tensor_tensor(out=lo[:, 1].rearrange("p (h d) -> p h d", d=LDV),
                                   in0=silu[:, 1].rearrange("p (h d) -> p h d", d=LDV), scalar=0.5,
                                   in1=gnorm[:].unsqueeze(1).broadcast_to([P, LH, LDV]), op0=ALU.mult,
                                   op1=ALU.mult).then_inc(v_ready, 1)
            dve.wait_ge(sq_ready, 1)
            link(V.tensor_reduce(lstat[:, 0], lo[:, 0].rearrange("p (h d) -> p h d", d=LDV), AX.X, ALU.add))
            V.tensor_scalar(lstat[:, 1], lstat[:, 0], 1.0 / LDV, LN_EPS, ALU.mult, ALU.add).then_inc(ms_ready, 1)
            dve.wait_ge(lr_ready, 1)
            link(V.tensor_tensor(lo[:, 2].rearrange("p (h d) -> p h d", d=LDV),
                                 ps[:, 2].rearrange("p (h d) -> p h d", d=LDV),
                                 lstat[:, 2].unsqueeze(2).broadcast_to([P, LH, LDV]), ALU.mult))
            dve.wait_ge(v_ready, 2)
            V.tensor_tensor(lo[:, 0], lo[:, 2], lo[:, 1], ALU.mult).then_inc(lo_ready, 1)
            dve.wait_ge(lw_psum, 1)
            link(V.tensor_tensor(x2[:], x1[:], ps[:, 4, 0:D], ALU.add))

            norm_stats(2, x2[:])
            normalise(2, xn[:], x2[:]).then_inc(xn_ready, 1)
            V.tensor_tensor(x2[:], x2[:], beta[:], ALU.add).then_inc(x2_ready, 1)
            dve.wait_ge(rl_psum, 1)
            logits = ps[:, 1, 0:E]
            link(V.max(rt[:, 0], logits))
            link(V.max_index(rt_idx[:], rt[:, 0], logits))
            V.tensor_scalar(rt[:, 1], rt[:, 0], rt[:, 0, 0:1], None, ALU.subtract).then_inc(rd_ready, 1)
            idx = rt[:, 4, 0:2]
            link(V.tensor_copy(idx, rt_idx[:, 0:2]))
            for k in range(2):
                V.tensor_scalar(pick[:, k], iota8, rt[:, 4, k:k + 1], None, ALU.is_equal).then_inc(pick_ready, 1)
            dve.wait_ge(loc_psum, 1)
            dve.wait_ge(pick_ready, 2)
            taken = rt[:, 5:7]
            link(V.tensor_tensor(taken, ps[:, 2, 0:2 * E].rearrange("p (k e) -> p k e", k=2), pick[:], ALU.mult))
            link(V.tensor_reduce(rt[:, 7, 0:2], taken, AX.X, ALU.add))
            link(V.tensor_scalar(rt[:, 8, 0:2], rt[:, 7, 0:2], float(CAP), None, ALU.is_lt))
            link(V.scalar_tensor_tensor(out=rt[:, 9, 0:2], in0=idx, scalar=float(SLOTS), in1=rt[:, 7, 0:2],
                                        op0=ALU.mult, op1=ALU.add))
            link(V.scalar_tensor_tensor(out=rt[:, 10, 0:2], in0=rt[:, 9, 0:2], scalar=1.0, in1=rt[:, 8, 0:2],
                                        op0=ALU.add, op1=ALU.mult))
            slot = [rt[:, 10, k:k + 1] for k in range(2)]
            link(V.tensor_scalar(onehot[:], slot_no, slot[0], None, ALU.is_equal))
            V.scalar_tensor_tensor(out=onehot[:], in0=slot_no, scalar=slot[1], in1=onehot[:], op0=ALU.is_equal,
                                   op1=ALU.add).then_inc(oh_ready, 1)
            dve.wait_ge(rexp_ready, 1)
            link(V.reciprocal(rt[:, 3, 1:2], rt[:, 3, 0:1]))
            link(V.tensor_scalar(rt[:, 11, 0:2], rt[:, 2, 0:2], rt[:, 3, 1:2], None, ALU.mult))
            link(V.tensor_reduce(rt[:, 12, 0:1], rt[:, 11, 0:2], AX.X, ALU.add))
            link(V.tensor_scalar(rt[:, 12, 1:2], rt[:, 12, 0:1], GATE_EPS, None, ALU.max))
            link(V.reciprocal(rt[:, 12, 2:3], rt[:, 12, 1:2]))
            link(V.tensor_scalar(rt[:, 13, 0:2], rt[:, 11, 0:2], rt[:, 12, 2:3], None, ALU.mult))
            dve.wait_ge(xd_psum, 1)
            V.tensor_copy(xd[:, 0], ps[:, 3]).then_inc(xd_ready, 1)
            dve.wait_ge(oh_ready, 1)
            link(V.tensor_scalar(gated[:], slot_no, slot[0], rt[:, 13, 0:1], ALU.is_equal, ALU.mult))
            dve.wait_ge(xd_psum, 2)
            link(V.tensor_scalar(onehot[:], slot_no, slot[1], rt[:, 13, 1:2], ALU.is_equal, ALU.mult))
            V.tensor_tensor(gated[:], gated[:], onehot[:], ALU.add).then_inc(gated_ready, 1)
            dve.wait_ge(zero_ready, 6)

            def bias_and_silu(n):
                for half in range(2):
                    chunks = slice(4 * half, 4 * half + 4)
                    dve.wait_ge(hidT_psum, 2 * n + half + 1)
                    if n >= 1:
                        dve.wait_ge(hT_ready, 2 * (n - 1) + half + 1)
                    bias = b1[:, 2 * n:2 * n + 2, chunks].rearrange("p e c -> p c e").unsqueeze(3)
                    V.tensor_tensor(hu[:, chunks],
                                    ps[:, 6 + half].rearrange("p (c e s) -> p c e s", c=4, e=2)[:, :, :, 0:CAP],
                                    bias.broadcast_to([P, 4, 2, CAP]), ALU.add).then_inc(hu_ready, 1)
                for half in range(2):
                    chunks = slice(4 * half, 4 * half + 4)
                    dve.wait_ge(ht_ready, 2 * n + half + 1)
                    if n >= 2:
                        dve.wait_ge(y_psum, n - 1)
                    V.scalar_tensor_tensor(out=hT[:, n % 2, chunks, :, 0:CAP], in0=ht[:, chunks], scalar=1.0,
                                           in1=hu[:, chunks], op0=ALU.add, op1=ALU.mult).then_inc(hT_ready, 1)

            def rows_out(n):
                dve.wait_ge(y_psum, n + 1)
                if n >= 2:
                    dve.wait_ge(c_psum, n - 1)
                V.scalar_tensor_tensor(out=ysb[:, n % 2], in0=ps[:, 2, 0:D], scalar=0.5, in1=b2[:, n],
                                       op0=ALU.mult, op1=ALU.add).then_inc(y_ready, 1)

            bias_and_silu(0)
            for n in range(1, E // 2):
                if n < E // 2 - 1:
                    rows_out(n - 1)
                    bias_and_silu(n)
                else:
                    rows_out(n - 1)
                    bias_and_silu(n)
            rows_out(E // 2 - 1)
            dve.wait_ge(c_psum, E // 2)
            link(V.tensor_tensor(fin[:, 0], xn[:], ps[:, 4, 0:D], ALU.add))
            norm_stats(3, fin[:, 0])
            link(normalise(3, fin[:, 1], fin[:, 0]))
            link(V.tensor_tensor(fin[:, 0], fin[:, 1], gamma[:], ALU.mult))
            dve.wait_ge(x2_ready, 1)
            V.tensor_tensor(fin[:, 2], fin[:, 0], x2[:], ALU.add).then_inc(out_ready, 1)

        @block.tensor
        def _(pe):
            MM = nc.tensor.matmul

            def transpose_xn(n):
                pe.wait_ge(xn_ready, n + 1)
                for c in range(DC):
                    last = nc.tensor.transpose(ps[:, 0, c * P:(c + 1) * P], xn[:, c * P:(c + 1) * P], eye)
                last.then_inc(xnT_psum, 1)

            def split_product(dst, lhs, rhs, start, stop):
                parts = [(0, 0), (0, 1), (1, 0)]
                for m, (i, j) in enumerate(parts):
                    last = MM(dst, lhs[i], rhs[j], start=start and m == 0, stop=stop and m == len(parts) - 1)
                return last

            def project_keys(kp):
                u, i = divmod(kp, KT)
                b, c, g = units[u]
                n = b * NC + c
                pe.wait_ge(ctxT_ready, n + 1)
                pe.wait_ge(wk_ready, DC * (g + 1))
                if kp >= 2:
                    pe.wait_ge(k_ready, kp - 1)
                for j in range(PK):
                    cols = slice((PK * i + j) * P, (PK * i + j + 1) * P)
                    for d in range(DC):
                        last = split_product(ps[:, K_BANK + kp % 2, j * CK:(j + 1) * CK],
                                             [w[:, g, d, cols] for w in (w_k_h, w_k_l)],
                                             [x[:, n % 2, d, :] for x in (ctxT_h, ctxT_l)], d == 0, d == DC - 1)
                last.then_inc(k_psum, 1)

            def scores(s):
                u, t = divmod(s, KT)
                b, c, g = units[u]
                pe.wait_ge(k_ready, KT * (u + 1))
                if s >= 2:
                    pe.wait_ge(e_ready, s - 1)
                for j in range(PG):
                    last = MM(ps[:, S_BANK + s % 2, j * P:(j + 1) * P], keys[:, u % 2, j, t * P:(t + 1) * P],
                              q_blk[:, g * PG + j, b, :], start=True, stop=True)
                last.then_inc(s_psum, 1)

            def weighted_sum(s):
                u, t = divmod(s, KT)
                b, c, g = units[u]
                n = b * NC + c
                pe.wait_ge(el_ready, s + 1)
                pe.wait_ge(ctx_ready, n + 1)
                if b == 1 and c == 0 and t == 0:
                    pe.wait_ge(mixT_ready, DC * (g + 1))
                for half in range(DC):
                    cols = slice(half * P, (half + 1) * P)
                    last = split_product(ps[:, mix_bank(half, g)], [x[:, n % 2, t, cols] for x in (ctx_h, ctx_l)],
                                         [x[:, s % NE, :] for x in (ex_h, ex_l)], c == 0 and t == 0,
                                         c == NC - 1 and t == KT - 1)
                last.then_inc(mix_done, 1)

            def denominators(g):
                pe.wait_ge(esum_ready, STEPS - (G - 1 - g) * KT)
                for j in range(PG):
                    for r in range(2):
                        h = HG * g + 2 * j + r
                        last = MM(ps[64 * r:64 * r + 64, den_bank(g), j * P:(j + 1) * P], ones[:, 0:DH],
                                  ex_sum[:, h].rearrange("p b q -> p (b q)"), start=True, stop=True)
                last.then_inc(den_psum, 1)

            def null_values(g):
                for j in range(PG):
                    MM(ps[:, value_bank(g), j * P:(j + 1) * P], null_v[:, (PG * g + j) * P:(PG * g + j + 1) * P],
                       null_ex[:], start=j == 0, stop=False, skip_group_check=True)

            def values(g):
                pe.wait_ge(mixT_ready, 2 * DC + g + 1)
                pe.wait_ge(mixT_half, g + 1)
                pe.wait_ge(ld_wv, 32)
                for j in range(PG):
                    for half in range(DC):
                        for r in range(2):
                            h = HG * g + 2 * j + r
                            last = MM(ps[64 * r:64 * r + 64, value_bank(g), j * P:(j + 1) * P],
                                      w_v[:, half, h * DH:(h + 1) * DH],
                                      mixT[:, half, h].rearrange("p b q -> p (b q)"), start=False,
                                      stop=j == PG - 1 and half == DC - 1, skip_group_check=True)
                last.then_inc(o_psum, 1)

            def output(g):
                pe.wait_ge(o_ready, g + 1)
                for n in range(4 * g, 4 * g + 4):
                    last = MM(ps[:, 2, 0:D], mixedT[:, n], w_out[:, n], start=n == 0, stop=n == FC - 1)
                if g == G - 1:
                    last.then_inc(wo_psum, 1)

            pe.wait_ge(ld_eye, 16)
            transpose_xn(0)
            project_keys(0)
            pe.wait_ge(xnT_ready, 1)
            pe.wait_ge(ld_wq, 16)
            for j in range(NPAIR):
                for c in range(DC):
                    last = MM(ps[:, 1 + j // 4, (j % 4) * P:(j % 4 + 1) * P], w_q[:, c, j * P:(j + 1) * P],
                              xnT[:, c], start=c == 0, stop=c == DC - 1)
                if j % 4 == 3:
                    last.then_inc(q_psum, 1)
            project_keys(1)
            pe.wait_ge(q_tanh, 2)
            pe.wait_ge(nk_tanh, 1)
            for j in range(NPAIR):
                last = MM(ps[0:H, 3, 0:P], null_kt[:, j], qT[:, j], start=j == 0, stop=j == NPAIR - 1)
            last.then_inc(null_psum, 1)
            project_keys(2)
            pe.wait_ge(q_ready, 4)
            LAG = 2
            for s in range(STEPS):
                if s == LAG:
                    pe.wait_ge(null_ready, 1)
                scores(s)
                if s + AHEAD < STEPS:
                    project_keys(s + AHEAD)
                if s >= LAG:
                    weighted_sum(s - LAG)
            pe.wait_ge(k_ready, STEPS)
            denominators(0)
            pe.wait_ge(ld_null_v, 16)
            null_values(0)
            weighted_sum(STEPS - 2)
            values(0)
            weighted_sum(STEPS - 1)
            pe.wait_ge(e_ready, STEPS)
            denominators(1)
            null_values(1)
            output(0)
            values(1)
            output(1)

            transpose_xn(1)
            pe.wait_ge(xnT_ready, 2)
            pe.wait_ge(ld_lin, 16 * 8)
            pe.wait_ge(ld_const, 16)
            for c in range(DC):
                last = MM(ps[0:LR, 2, 0:P], w_gk1[:, c], xnT[:, c], start=c == 0, stop=c == DC - 1)
            last.then_inc(low_psum, 1)
            for w, weight in enumerate((w_lq, w_lk)):
                for j in range(2):
                    for c in range(DC):
                        last = MM(ps[:, 1, (2 * w + j) * P:(2 * w + j + 1) * P], weight[:, c, j * P:(j + 1) * P],
                                  xnT[:, c], start=c == 0, stop=c == DC - 1)
            last.then_inc(qk_psum, 1)
            pe.wait_ge(low_ready, 1)
            MM(ps[:, 3, 0:LH * LDK], lowT[0:LR + 1], w_gk2[0:LR + 1], start=True, stop=True).then_inc(logit_psum, 1)
            for c in range(DC):
                last = MM(ps[:, 4], xnT[:, c], w_lv[:, c], start=c == 0, stop=c == DC - 1)
            last.then_inc(v_psum, 1)
            for c in range(DC):
                last = MM(ps[:, 5], xnT[:, c], w_lg[:, c], start=c == 0, stop=c == DC - 1)
            last.then_inc(g_psum, 1)
            pe.wait_ge(g_ready, 1)
            for pair in range(2):
                bank = (6, 2)[pair]
                lhs = gate[:, 3, pair * P:(pair + 1) * P]
                MM(ps[:, bank], lhs, const[:, C_DECAY:C_DECAY + 512], start=True, stop=True)
                MM(ps[:, bank + 1, 0:NL * P - 512], lhs, const[:, C_DECAY + 512:C_DECAY + NL * P], start=True,
                   stop=True).then_inc(dec_psum, 1)
            pe.wait_ge(qk_ready, 3)
            for pair in range(2):
                last = MM(ps[:, 0, 2 * pair * P:2 * (pair + 1) * P], lkT[:, pair], lqT[:, pair], start=True, stop=True)
            last.then_inc(lev_psum, 1)
            pe.wait_ge(kx_ready, 2)
            pe.wait_ge(dec_ready, 2)
            for n in range(NL):
                pe.wait_ge(qx_ready, NL + n + 1)
                for pair in range(2):
                    at = 256 * (n % 2) + 128 * pair
                    last = MM(ps[:, (1, 6, 7)[n // 2], at:at + 128], kx[:, pair, n], qx[:, pair, n], start=True,
                              stop=True)
                if n % 2:
                    last.then_inc(lev_psum, 1)
            pe.wait_ge(att_ready, 1)
            pe.wait_ge(v_ready, 1)
            for h in range(LH):
                last = MM(ps[:, 2, h * LDV:(h + 1) * LDV], att[:, h], lv[:, h * LDV:(h + 1) * LDV], start=True,
                          stop=True)
            last.then_inc(lo_psum, 1)
            pe.wait_ge(lo_ready, 1)
            for h in range(LH):
                last = nc.tensor.transpose(ps[:, 3, h * P:(h + 1) * P], lo[:, 0, h * P:(h + 1) * P], eye)
            last.then_inc(loT_psum, 1)
            pe.wait_ge(loT_ready, 1)
            for h in range(LH):
                last = MM(ps[:, 4, 0:D], loT[:, h], w_lo[:, h], start=h == 0, stop=h == LH - 1)
            last.then_inc(lw_psum, 1)

            transpose_xn(2)
            pe.wait_ge(xnT_ready, 3)
            for c in range(DC):
                last = MM(ps[:, 1, 0:E], xnT[:, c], w_route[:, c], start=c == 0, stop=c == DC - 1)
            last.then_inc(rl_psum, 1)
            pe.wait_ge(pick_ready, 2)
            MM(ps[:, 2, 0:2 * E], strict, pick[:].rearrange("p k e -> p (k e)"), start=True, stop=False,
               skip_group_check=True)
            MM(ps[:, 2, E:2 * E], ones, pick[:, 0], start=False, stop=True, skip_group_check=True).then_inc(loc_psum, 1)
            pe.wait_ge(oh_ready, 1)
            for c in range(DC):
                MM(ps[:, (3, 5)[c]], xn[:, c * P:(c + 1) * P], onehot[:], start=True, stop=True).then_inc(xd_psum, 1)
            pe.wait_ge(xd_ready, 2)

            def up(n):
                for j in range(2):
                    pe.wait_ge(ld_exp[2 * n + j], 32)
                for half in range(2):
                    if n:
                        pe.wait_ge(hid_ready, 2 * (n - 1) + half + 1)
                    for c in range(DC):
                        for j in range(2):
                            e = 2 * n + j
                            last = MM(ps[SLOTS * j:SLOTS * (j + 1), half], xd[:, c, e * SLOTS:(e + 1) * SLOTS],
                                      w1[e][:, c, half * 512:(half + 1) * 512], start=c == 0, stop=c == DC - 1)
                    last.then_inc(f1_psum, 1)

            def turn(n):
                for half in range(2):
                    pe.wait_ge(hid_ready, 2 * n + half + 1)
                    if n:
                        pe.wait_ge(hu_ready, 2 * (n - 1) + half + 1)
                    for c in range(4):
                        last = nc.tensor.transpose(ps[:, 6 + half, c * P:(c + 1) * P],
                                                   hid[:, (4 * half + c) * P:(4 * half + c + 1) * P], eye)
                    last.then_inc(hidT_psum, 1)

            def down(n):
                pe.wait_ge(hT_ready, 2 * n + 2)
                if n:
                    pe.wait_ge(y_ready, n)
                for c in range(FC):
                    for j in range(2):
                        last = MM(ps[SLOTS * j:SLOTS * (j + 1), 2, 0:D], hT[:, n % 2, c, j], w2[2 * n + j][:, c],
                                  start=c == 0, stop=c == FC - 1)
                last.then_inc(y_psum, 1)

            def combine(n):
                pe.wait_ge(y_ready, n + 1)
                if n == 0:
                    pe.wait_ge(gatedT_ready, 1)
                MM(ps[:, 4, 0:D], gatedT[:, n], ysb[:, n % 2], start=n == 0, stop=n == E // 2 - 1).then_inc(c_psum, 1)

            up(0)
            turn(0)
            pe.wait_ge(gated_ready, 1)
            for n in range(E // 2):
                last = nc.tensor.transpose(ps[:, 3, n * P:(n + 1) * P], gated[:, n * P:(n + 1) * P], eye)
            last.then_inc(gatedT_psum, 1)
            up(1)
            down(0)
            turn(1)
            up(2)
            combine(0)
            down(1)
            turn(2)
            up(3)
            turn(3)
            combine(1)
            down(2)
            combine(2)
            down(3)
            combine(3)


_PLAIN = {
    "Wq": "L0_xattn_Wq", "Wkv": "L0_xattn_Wkv", "Wout": "L0_xattn_Wout", "bout": "L0_xattn_bout",
    "lWq": "L0_attn_Wq", "lWk": "L0_attn_Wk", "lWv": "L0_attn_Wv", "lWg": "L0_attn_Wg", "lWo": "L0_attn_Wo",
    "Wgk1": "L0_attn_Wgk1", "gnorm": "L0_attn_g_norm_weight", "wg": "L0_ffn_wg", "fc2": "L0_ffn_fc2_w",
    "b2": "L0_ffn_fc2_b", "gamma": "L0_ffn_ln_gamma", "beta": "L0_ffn_ln_beta",
}


def kernel(**inputs):
    import concourse.bacc as _bacc
    from concourse.bass_utils import run_bass_kernel_spmd as _run

    v = {k: np.ascontiguousarray(x) for k, x in inputs.items()}
    arrays = {short: v[name] for short, name in _PLAIN.items()}
    arrays["x"] = v["x"].reshape(P, D)
    arrays["ctx"] = v["ctx_1024"].reshape(B * NK, D)
    arrays["ctxT"] = arrays["ctx"].T
    arrays["Wgk2b"] = np.concatenate([v["L0_attn_Wgk2"], v["L0_attn_bgk2"][None, :]])
    arrays["fc1T"] = v["L0_ffn_fc1_w"].transpose(0, 2, 1)
    arrays["b1"] = v["L0_ffn_fc1_b"].reshape(E, FC, P).transpose(2, 0, 1)
    null_k = np.zeros((P, NPAIR, H), np.float32)
    null_v = np.zeros((H, INNER), np.float32)
    for h in range(H):
        rows = slice(DH * (h % 2), DH * (h % 2) + DH)
        null_k[rows, h // 2, h] = v["L0_xattn_null_key"]
        null_v[h, h * DH:(h + 1) * DH] = v["L0_xattn_null_value"]
    arrays["null_k"], arrays["null_v"] = null_k, null_v
    arrays["const"] = shape_constants()

    nc = _bacc.Bacc("TRN2", target_bir_lowering=False, num_devices=1)
    feed, a = {}, {}
    for name, x in arrays.items():
        feed[f"in_{name}"] = x = np.ascontiguousarray(x)
        a[name] = nc.dram_tensor(f"in_{name}", x.shape, mybir.dt.from_np(x.dtype), kind="ExternalInput").ap()
    out = nc.dram_tensor("out_x", (P, D), F32, kind="ExternalOutput").ap()
    block_kernel(nc, a, out)
    r = _run(nc, [feed], core_ids=[0])
    return r.results[0]["out_x"].reshape(B, S, D)
```

```python
from contextlib import ExitStack

import numpy as np

import concourse.bass as bass
from concourse import mybir

F32 = mybir.dt.float32
F32R = mybir.dt.float32r
BF16 = mybir.dt.bfloat16
U32 = mybir.dt.uint32
ALU = mybir.AluOpType
ACT = mybir.ActivationFunctionType
AX = mybir.AxisListType

P = 128
B, S, D = 2, 64, 256
NK = 1024
H, DH = 16, 64
INNER = H * DH
DC = D // P
CK = 256
NC = NK // CK
KT = CK // P
G = 2
HG = H // G
PG = HG // 2
NPAIR = H // 2
PK = PG // KT
LH, LDK, LDV, LR = 4, 64, 128, 16
LEVELS = [32, 16, 8, 4, 2, 1]
NL = len(LEVELS)
GATE_NORM = 16.0
E, FH = 8, 1024
FC = FH // P
N_TOK = B * S
CAP = 2 * int(1.25 * ((N_TOK + E - 1) // E))
SLOTS = 64
LN_EPS = 1e-5
GATE_EPS = 1.1920929e-07
assert B * S == P and CAP <= SLOTS

C_EYE, C_ONES, C_STRICT, C_IOTA8, C_FIRST, C_MASK, C_DECAY, C_SLOT = 0, 128, 256, 384, 392, 400, 784, 1552
C_WIDTH = C_SLOT + E * SLOTS


def shape_constants():
    c = np.zeros((P, C_WIDTH), np.float32)
    t = np.arange(P)
    c[:, C_EYE:C_EYE + P] = np.eye(P)
    c[:, C_STRICT:C_STRICT + P] = t[:, None] < t[None, :]
    c[:, C_ONES:C_ONES + P] = 1.0
    c[:, C_IOTA8:C_IOTA8 + E] = np.arange(E)
    c[:, C_FIRST:C_FIRST + E] = np.arange(E) * SLOTS + 1
    for n, half in enumerate(LEVELS):
        block, right = t // (2 * half), t // half % 2 == 1
        edge = block * 2 * half + half
        cols = t[right]
        same = block[:, None] == block[None, cols]
        c[:, C_MASK + n * 64:C_MASK + (n + 1) * 64] = same & ~right[:, None]
        u, at = t[:, None], t[None, :]
        in_right = (u >= edge[None, :]) & (u <= at)
        in_left = (u > at) & (u < edge[None, :])
        c[:, C_DECAY + n * P:C_DECAY + (n + 1) * P] = np.where(right[None, :], in_right, in_left)
    c[:, C_SLOT:] = np.arange(1, E * SLOTS + 1)
    return c


def block_kernel(nc, a, out):
    with ExitStack() as whole:
        def sem(name):
            return whole.enter_context(nc.semaphore(name))

        def alloc(stack, name, shape, dt=F32):
            return stack.enter_context(nc.sbuf_tensor(name, shape, dt))

        ps = whole.enter_context(nc.psum_tensor("ps", [P, 8, 512], F32))

        def keep(name, shape, dt=F32):
            return alloc(whole, name, shape, dt)

        const = keep("const", [P, C_WIDTH])
        eye = const[:, C_EYE:C_EYE + P]
        strict = const[:, C_STRICT:C_STRICT + P]
        ones = const[:, C_ONES:C_ONES + P]
        iota8 = const[:, C_IOTA8:C_IOTA8 + E]
        first_slot = const[:, C_FIRST:C_FIRST + E]
        slot_no = const[:, C_SLOT:C_SLOT + E * SLOTS]
        minus_half = keep("minus_half", [P, LH])
        warmer = keep("warmer", [P, 512], BF16)
        strict_b = keep("strict_b", [P, P], BF16)
        ones_b = keep("ones_b", [P, P], BF16)
        x0 = keep("x0", [P, D])
        x1 = keep("x1", [P, D])
        x2 = keep("x2", [P, D])
        xn = keep("xn", [P, D])
        xnT = keep("xnT", [P, DC, P])
        bout = keep("bout", [P, D])
        gamma = keep("gamma", [P, D])
        beta = keep("beta", [P, D])
        gnorm = keep("gnorm", [P, LDV])
        stat = keep("stat", [P, 4, 16])
        w_lq = keep("w_lq", [P, DC, LH * LDK])
        w_lk = keep("w_lk", [P, DC, LH * LDK])
        w_lv = keep("w_lv", [P, DC, LH * LDV])
        w_lg = keep("w_lg", [P, DC, LH * LDV])
        w_lo = keep("w_lo", [P, LH, D])
        w_gk1 = keep("w_gk1", [P, DC, LR])
        w_gk2 = keep("w_gk2", [32, LH * LDK])
        w_route = keep("w_route", [P, DC, E])
        b1 = keep("b1", [P, E, FC])
        b2 = keep("b2", [P, E // 2, D])

        attn_a = ExitStack()
        w_k_stage = alloc(attn_a, "w_k_stage", [P, G, DC, INNER // G])
        stage_t = alloc(attn_a, "stage_t", [P, 2, DC, CK])
        stage_n = alloc(attn_a, "stage_n", [P, 2, KT, D])
        w_k_h = alloc(attn_a, "w_k_h", [P, G, DC, INNER // G], F32R)
        w_k_l = alloc(attn_a, "w_k_l", [P, G, DC, INNER // G], F32R)
        ctxT_h = alloc(attn_a, "ctxT_h", [P, 2, DC, CK], F32R)
        ctxT_l = alloc(attn_a, "ctxT_l", [P, 2, DC, CK], F32R)
        keys = alloc(attn_a, "keys", [P, 2, PG, CK])
        ctx_h = alloc(attn_a, "ctx_h", [P, 2, KT, D], F32R)
        ctx_l = alloc(attn_a, "ctx_l", [P, 2, KT, D], F32R)
        NE = 4
        ex = alloc(attn_a, "ex", [P, NE, 512])
        ex_h = alloc(attn_a, "ex_h", [P, NE, 512], F32R)
        ex_l = alloc(attn_a, "ex_l", [P, NE, 512], F32R)
        q_blk = alloc(attn_a, "q_blk", [P, NPAIR, B, P])
        null_k = alloc(attn_a, "null_k", [P, P])
        null_kt = alloc(attn_a, "null_kt", [P, P])
        qT = alloc(attn_a, "qT", [P, NPAIR, P])
        alloc(attn_a, "rest_of_seven_experts", [P, 4864])
        attn_b = ExitStack()
        w_v = alloc(attn_b, "w_v", [P, DC, INNER])
        w_out = alloc(attn_b, "w_out", [P, FC, D])
        mixT = alloc(attn_b, "mixT", [P, DC, H, B, S])
        ex_sum = alloc(attn_b, "ex_sum", [P, H, B, S])
        w_q = mixT[:, 0].rearrange("p h b s -> p (h b s)").rearrange("p (c n) -> p c n", c=DC)
        null_v = alloc(attn_b, "null_v", [P, 1])
        null_ex = alloc(attn_b, "null_ex", [P, NPAIR, P])
        mixedT = alloc(attn_b, "mixedT", [P, FC, P])
        share = alloc(attn_b, "share", [P, G, PG, P])
        attn_b.close()
        attn_a.close()

        w1, w2 = [], []
        for e in range(E):
            w1.append(keep(f"w1_{e}", [P, DC, FH]))
            w2.append(keep(f"w2_{e}", [P, FC, D]))

        lin = ExitStack()
        lqT = alloc(lin, "lqT", [P, 2, 2, P])
        lkT = alloc(lin, "lkT", [P, 2, P])
        lowT = alloc(lin, "lowT", [32, P])
        gate = alloc(lin, "gate", [P, 4, LH * LDK])
        lv = alloc(lin, "lv", [P, LH * LDV])
        silu = alloc(lin, "silu", [P, 2, LH * LDV])
        decay = alloc(lin, "decay", [P, 2, NL, P])
        kx = alloc(lin, "kx", [P, 2, NL, P])
        qx = alloc(lin, "qx", [P, 2, NL, 2, 64])
        att = alloc(lin, "att", [P, LH, P])
        lo = alloc(lin, "lo", [P, 3, LH * LDV])
        loT = decay[:, 0, 0:LH]
        lstat = alloc(lin, "lstat", [P, 4, LH])
        lin.close()

        moe = whole
        top = alloc(moe, "top", [P, E])
        top_idx = alloc(moe, "top_idx", [P, E], U32)
        below = alloc(moe, "below", [P, E])
        top_exp = alloc(moe, "top_exp", [P, E])
        gate_sum = alloc(moe, "gate_sum", [P, 4])
        gates = alloc(moe, "gates", [P, 2])
        pick = alloc(moe, "pick", [P, 2, E], BF16)
        kept = alloc(moe, "kept", [P, 2, E])
        place = alloc(moe, "place", [P, 2, E])
        picked = alloc(moe, "picked", [P, 2, E])
        slot = alloc(moe, "slot", [P, 2])
        xn_h = alloc(moe, "xn_h", [P, D], F32R)
        xn_l = alloc(moe, "xn_l", [P, D], F32R)
        onehot = alloc(moe, "onehot", [P, E * SLOTS], F32R)
        gated = alloc(moe, "gated", [P, 2, E * SLOTS])
        gatedT = alloc(moe, "gatedT", [P, E // 2, P])
        xd = alloc(moe, "xd", [P, DC, E * SLOTS])
        hid = alloc(moe, "hid", [P, FH])
        hu = alloc(moe, "hu", [P, FC, 2, CAP])
        ht = alloc(moe, "ht", [P, FC, 2, CAP])
        hT = alloc(moe, "hT", [P, 2, FC, 2, SLOTS])
        ysb = alloc(moe, "ysb", [P, 2, D])
        fin = alloc(moe, "fin", [P, 2, D])

        ld_x = sem("ld_x")
        ld_eye = sem("ld_eye")
        ld_const = sem("ld_const")
        null_sums = sem("null_sums")
        null_values = sem("null_values")
        half_ready = sem("half_ready")
        warmer_ready = sem("warmer_ready")
        ld_wq = [sem(f"ld_wq{half}") for half in range(2)]
        ld_wk = [sem(f"ld_wk{i}") for i in range(G * KT)]
        ld_ctx = [sem(f"ld_ctx{n}") for n in range(B * NC)]
        ld_ctxT = [sem(f"ld_ctxT{n}") for n in range(B * NC)]
        ld_null = sem("ld_null")
        ld_null_v = sem("ld_null_v")
        ld_wv = sem("ld_wv")
        ld_lin = sem("ld_lin")
        ld_small = sem("ld_small")
        ld_exp = [sem(f"ld_exp{e}") for e in range(E)]
        st_out = sem("st_out")
        dve_seq = sem("dve_seq")
        act_seq = sem("act_seq")
        var_ready = sem("var_ready")
        rstd_ready = sem("rstd_ready")
        xn_ready = sem("xn_ready")
        xnT_psum = sem("xnT_psum")
        xnT_ready = sem("xnT_ready")
        zero_ready = sem("zero_ready")
        q_blk_zero = sem("q_blk_zero")
        q_psum = sem("q_psum")
        q_tanh = sem("q_tanh")
        q_ready = sem("q_ready")
        nk_tanh = sem("nk_tanh")
        null_psum = sem("null_psum")
        null_ready = sem("null_ready")
        wk_high = sem("wk_high")
        wk_ready = sem("wk_ready")
        ctxT_high = sem("ctxT_high")
        ctxT_ready = sem("ctxT_ready")
        ctx_ready = sem("ctx_ready")
        k_psum = sem("k_psum")
        k_ready = sem("k_ready")
        s_psum = sem("s_psum")
        e_ready = sem("e_ready")
        el_ready = sem("el_ready")
        esum_ready = sem("esum_ready")
        mix_done = sem("mix_done")
        mixT_ready = sem("mixT_ready")
        mixT_last = sem("mixT_last")
        den_psum = sem("den_psum")
        share_ready = sem("share_ready")
        o_psum = sem("o_psum")
        o_ready = sem("o_ready")
        wo_psum = sem("wo_psum")
        x0_ready = sem("x0_ready")
        x1_ready = sem("x1_ready")
        low_psum = sem("low_psum")
        low_ready = sem("low_ready")
        logit_psum = sem("logit_psum")
        qk_psum = sem("qk_psum")
        qk_ready = sem("qk_ready")
        v_psum = sem("v_psum")
        v_ready = sem("v_ready")
        g_psum = sem("g_psum")
        gln_ready = sem("gln_ready")
        g_ready = sem("g_ready")
        dec_psum = sem("dec_psum")
        dec_ready = sem("dec_ready")
        gtanh_ready = sem("gtanh_ready")
        kx_ready = sem("kx_ready")
        kx_pool = sem("kx_pool")
        gain_ready = sem("gain_ready")
        own_psum = sem("own_psum")
        qx_ready = sem("qx_ready")
        lev_psum = sem("lev_psum")
        att_ready = sem("att_ready")
        lo_psum = sem("lo_psum")
        sq_ready = sem("sq_ready")
        ms_ready = sem("ms_ready")
        lr_ready = sem("lr_ready")
        lo_ready = sem("lo_ready")
        loT_psum = sem("loT_psum")
        loT_ready = sem("loT_ready")
        lw_psum = sem("lw_psum")
        x2_ready = sem("x2_ready")
        rl_psum = sem("rl_psum")
        below_ready = sem("below_ready")
        top_exp_ready = sem("top_exp_ready")
        triangle_ready = sem("triangle_ready")
        xn_split = sem("xn_split")
        pick_ready = sem("pick_ready")
        loc_psum = sem("loc_psum")
        oh_ready = sem("oh_ready")
        xd_psum = sem("xd_psum")
        xd_ready = sem("xd_ready")
        gated_ready = sem("gated_ready")
        gatedT_psum = sem("gatedT_psum")
        gatedT_ready = sem("gatedT_ready")
        f1_psum = sem("f1_psum")
        hid_ready = sem("hid_ready")
        hidT_psum = sem("hidT_psum")
        hu_ready = sem("hu_ready")
        ht_ready = sem("ht_ready")
        hT_ready = sem("hT_ready")
        y_psum = sem("y_psum")
        y_ready = sem("y_ready")
        c_psum = sem("c_psum")
        out_ready = sem("out_ready")

        units = [(b, c, g) for b in range(B) for c in range(NC) for g in range(G)]
        NU = len(units)
        STEPS = NU * KT
        AHEAD = KT + 1

        def mix_bank(half, g):
            return 2 * half + g
        K_BANK, S_BANK = 4, 6
        NULL_BANK = (3, 0)
        Y_BANK = (2, 5)

        def den_bank(g):
            return (4, 6)[g]

        def value_bank(g):
            return (5, 7)[g]

        def w_k_piece(w, i):
            return w[:, i // KT, :, (i % KT) * PK * P:(i % KT + 1) * PK * P]

        block = whole.enter_context(nc.Block())

        @block.sync
        def _(sp):
            def load_ctxT(n):
                if n >= 2:
                    sp.wait_ge(ctxT_ready, n - 1)
                cols = slice(n * CK, (n + 1) * CK)
                sp.dma_start(stage_t[:, n % 2], a["ctxT"][:, cols].rearrange("(c p) n -> p c n", p=P)).then_inc(ld_ctxT[n], 16)

            def load_ctx(n):
                if n >= 2:
                    sp.wait_ge(ctx_ready, n - 1)
                rows = slice(n * CK, (n + 1) * CK)
                sp.dma_start(stage_n[:, n % 2], a["ctx"][rows].rearrange("(t p) d -> p t d", p=P)).then_inc(ld_ctx[n], 16)

            def load_wk(i):
                sp.dma_start(w_k_piece(w_k_stage, i),
                             a["Wkv"][:, i * PK * P:(i + 1) * PK * P].rearrange("(c p) n -> p c n", p=P)).then_inc(ld_wk[i], 16)

            def chunked(name, p=P):
                return a[name].rearrange("(c p) n -> p c n", p=p)

            def in_each_row(name):
                return a[name].rearrange("(o d) -> o d", o=1).broadcast_to([P, a[name].shape[0]])

            sp.dma_start(x0[:], a["x"]).then_inc(ld_x, 16)
            sp.dma_start(const[:, 0:C_STRICT], a["const"][:, 0:C_STRICT]).then_inc(ld_eye, 16)
            load_wk(0)
            load_ctxT(0)
            for half in range(2):
                cols = slice(half * 512, (half + 1) * 512)
                sp.dma_start(w_q[:, :, cols], chunked("Wq")[:, :, cols]).then_inc(ld_wq[half], 16)
            load_wk(1)
            sp.dma_start(null_k[:], a["null_k"]).then_inc(ld_null, 16)
            sp.dma_start(null_v[:], a["null_v"]).then_inc(ld_null_v, 16)
            load_wk(2)
            load_wk(3)
            load_ctx(0)
            load_ctxT(1)
            load_ctx(1)
            sp.dma_start(const[:, C_STRICT:], a["const"][:, C_STRICT:]).then_inc(ld_const, 16)
            sp.dma_start(bout[:], in_each_row("bout")).then_inc(ld_small, 16)
            sp.dma_start(gamma[:], in_each_row("gamma")).then_inc(ld_small, 16)
            sp.dma_start(beta[:], in_each_row("beta")).then_inc(ld_small, 16)
            sp.dma_start(gnorm[:], in_each_row("gnorm")).then_inc(ld_small, 16)
            sp.dma_start(b1[:], a["b1"]).then_inc(ld_small, 16)
            for e in range(E):
                half = SLOTS * (e % 2)
                sp.dma_start(b2[half:half + SLOTS, e // 2, :],
                             a["b2"][e:e + 1, :].broadcast_to([SLOTS, D])).then_inc(ld_small, 16)
            sp.dma_start(w_v[:], a["Wkv"][:, INNER:2 * INNER].rearrange("(c p) n -> p c n", p=P)).then_inc(ld_wv, 16)
            sp.dma_start(w_out[:], chunked("Wout")).then_inc(ld_wv, 16)
            load_ctxT(2)
            load_ctx(2)
            sp.dma_start(w_lq[:], chunked("lWq")).then_inc(ld_lin, 16)
            sp.dma_start(w_lk[:], chunked("lWk")).then_inc(ld_lin, 16)
            sp.dma_start(w_lv[:], chunked("lWv")).then_inc(ld_lin, 16)
            sp.dma_start(w_lg[:], chunked("lWg")).then_inc(ld_lin, 16)
            sp.dma_start(w_lo[:], chunked("lWo")).then_inc(ld_lin, 16)
            sp.dma_start(w_gk1[:], chunked("Wgk1")).then_inc(ld_lin, 16)
            sp.dma_start(w_gk2[0:LR + 1], a["Wgk2b"]).then_inc(ld_lin, 16)
            sp.dma_start(w_route[:], chunked("wg")).then_inc(ld_lin, 16)
            for n in range(3, B * NC):
                load_ctxT(n)
                load_ctx(n)
            for e in range(E):
                if e == 0:
                    sp.wait_ge(ctx_ready, B * NC)
                if e == 1:
                    sp.wait_ge(k_psum, STEPS)
                if e == 2:
                    sp.wait_ge(mix_done, STEPS)
                    sp.wait_ge(esum_ready, STEPS)
                if e == 7:
                    sp.wait_ge(wo_psum, 1)
                sp.dma_start(w1[e][:], a["fc1T"][e].rearrange("(c p) n -> p c n", p=P)).then_inc(ld_exp[e], 16)
                sp.dma_start(w2[e][:], a["fc2"][e].rearrange("(c p) n -> p c n", p=P)).then_inc(ld_exp[e], 16)
            sp.wait_ge(out_ready, 1)
            sp.dma_start(out, fin[:, 1, :]).then_inc(st_out, 16)
            sp.wait_ge(st_out, 16)

        @block.gpsimd
        def _(pool):
            nc.gpsimd.memset(warmer[:], 0.5).then_inc(warmer_ready, 1)
            nc.gpsimd.memset(minus_half[:], -0.5).then_inc(half_ready, 1)
            pool.wait_ge(half_ready, 1)
            for n in range(3):
                pool.wait_ge(var_ready, n + 1)
                nc.gpsimd.tensor_tensor(stat[:, n, 9:10], stat[:, n, 8:9], minus_half[:, 0:1], ALU.pow).then_inc(rstd_ready, 1)
                if n == 0:
                    nc.gpsimd.memset(ex_sum[:], 0.0).then_inc(zero_ready, 1)
                    pool.wait_ge(zero_ready, 1)
                    pool.wait_ge(null_ready, 2)
                    for r in range(2):
                        row = slice(64 * r, 64 * r + 1)
                        heads = ex_sum[row].rearrange("p (j r) b q -> p r j (b q)", r=2)[:, r]
                        nc.gpsimd.tensor_copy(heads, null_ex[row]).then_inc(null_sums, 1)
                    pool.wait_ge(null_sums, 2)
                    pool.wait_ge(ld_null_v, 16)
                    nc.gpsimd.tensor_scalar(null_ex[:], null_ex[:], null_v[:], None, ALU.mult).then_inc(null_values, 1)
                    pool.wait_ge(ld_const, 16)
                    nc.gpsimd.tensor_copy(strict_b[:], strict).then_inc(triangle_ready, 1)
                    nc.gpsimd.tensor_copy(ones_b[:], ones).then_inc(triangle_ready, 1)
                    pool.wait_ge(wo_psum, 1)
                    nc.gpsimd.memset(lowT[:], 1.0).then_inc(zero_ready, 1)
                    nc.gpsimd.memset(lqT[:], 0.0).then_inc(zero_ready, 1)
                if n == 1:
                    pool.wait_ge(qk_ready, 3)
                    for pair, first, last in ((1, 0, 4), (0, 4, NL), (1, 4, NL)):
                        pool.wait_ge(dec_ready, 2 if first == 0 else 3)
                        nc.gpsimd.tensor_tensor(kx[:, pair, first:last], decay[:, pair, first:last],
                                                lkT[:, pair].unsqueeze(1).broadcast_to([P, last - first, P]),
                                                ALU.mult).then_inc(kx_pool, 1)
                    pool.wait_ge(ms_ready, 1)
                    nc.gpsimd.tensor_tensor(lstat[:, 2], lstat[:, 1], minus_half[:], ALU.pow).then_inc(lr_ready, 1)
                if n == 2:
                    nc.gpsimd.memset(hT[:], 0.0).then_inc(zero_ready, 1)
            pool.wait_ge(var_ready, 4)
            nc.gpsimd.tensor_tensor(stat[:, 3, 9:10], stat[:, 3, 8:9], minus_half[:, 0:1], ALU.pow).then_inc(rstd_ready, 1)

        @block.scalar
        def _(act):
            seq = [0]

            def link(ins):
                seq[0] += 1
                ins.then_inc(act_seq, 1)
                act.wait_ge(act_seq, seq[0])

            def copy(dst, src, done):
                nc.scalar.activation(dst, src, ACT.Copy).then_inc(done, 1)

            def split_wk(i):
                act.wait_ge(ld_wk[i], 16)
                copy(w_k_piece(w_k_h, i), w_k_piece(w_k_stage, i), wk_high)

            def keys_tanh(kp):
                u, i = divmod(kp, KT)
                act.wait_ge(k_psum, kp + 1)
                if u >= 2:
                    act.wait_ge(s_psum, KT * (u - 1))
                src = ps[:, K_BANK + kp % 2].rearrange("p (j n) -> p j n", j=PK)
                nc.scalar.activation(keys[:, u % 2, PK * i:PK * (i + 1)], src, ACT.Tanh).then_inc(k_ready, 1)

            split_wk(0)
            act.wait_ge(ld_ctxT[0], 16)
            copy(ctxT_h[:, 0], stage_t[:, 0], ctxT_high)
            split_wk(1)
            act.wait_ge(ld_null, 16)
            nc.scalar.activation(null_kt[:], null_k[:], ACT.Tanh).then_inc(nk_tanh, 1)
            keys_tanh(0)
            for j in range(2):
                act.wait_ge(q_psum, j + 1)
                src = ps[:, 1 + j].rearrange("p (j t) -> p j t", t=P)
                nc.scalar.activation(qT[:, 4 * j:4 * j + 4], src, ACT.Tanh).then_inc(q_tanh, 1)
                split_wk(2 + j)
            keys_tanh(1)
            keys_tanh(2)
            for j in range(2):
                act.wait_ge(null_psum, j + 1)
                nc.scalar.activation(null_ex[:, 4 * j:4 * j + 4], ps[:, NULL_BANK[j]].rearrange("p (j t) -> p j t", t=P),
                                     ACT.Exp, scale=DH ** -0.5).then_inc(null_ready, 1)

            for s in range(STEPS):
                act.wait_ge(s_psum, s + 1)
                r = s % NE
                if s >= NE:
                    act.wait_ge(esum_ready, s - NE + 1)
                    act.wait_ge(mix_done, s - NE + 1)
                nc.scalar.activation(ex[:, r], ps[:, S_BANK + s % 2], ACT.Exp, scale=DH ** -0.5)
                nc.scalar.activation(ex_h[:, r], ps[:, S_BANK + s % 2], ACT.Exp, scale=DH ** -0.5).then_inc(e_ready, 1)
                if s + AHEAD < STEPS:
                    keys_tanh(s + AHEAD)
            act.preload_act_table_set("natural_log_exp_and_others")
            for g in range(G):
                act.wait_ge(mix_done, STEPS - (G - 1 - g) * KT)
                for half in range(DC):
                    copy(mixT[:, half, HG * g:HG * (g + 1), B - 1, :],
                         ps[:, mix_bank(half, g)].rearrange("p (h q) -> p h q", q=S), mixT_last)

            act.wait_ge(xnT_psum, 2)
            copy(xnT[:], ps[:, 0, 0:DC * P].rearrange("p (c t) -> p c t", c=DC), xnT_ready)
            act.wait_ge(logit_psum, 1)
            link(nc.scalar.activation(gate[:, 0], ps[:, 3, D:2 * D], ACT.Abs))
            link(nc.scalar.activation(gate[:, 1], gate[:, 0], ACT.Exp, scale=-1.0))
            nc.scalar.activation(gate[:, 2], gate[:, 1], ACT.Ln, bias=1.0).then_inc(gln_ready, 1)
            for pair in range(2):
                act.wait_ge(dec_psum, pair + 1)
                nc.scalar.activation(decay[:, pair, 0:4], ps[:, 6 + pair].rearrange("p (l t) -> p l t", t=P), ACT.Exp,
                                     scale=1.0 / GATE_NORM).then_inc(dec_ready, 1)
            act.wait_ge(dec_psum, 3)
            nc.scalar.activation(decay[:, :, 4:NL], ps[:, 2].rearrange("p (j l t) -> p j l t", j=2, t=P), ACT.Exp,
                                 scale=1.0 / GATE_NORM).then_inc(dec_ready, 1)
            act.preload_act_table_set("exp_and_others")
            act.wait_ge(v_psum, 1)
            copy(lv[:], ps[:, 4], v_ready)
            act.wait_ge(g_psum, 1)
            nc.scalar.activation(silu[:, 0], ps[:, 5], ACT.Tanh, scale=0.5).then_inc(gtanh_ready, 1)
            for h in range(LH):
                act.wait_ge(lo_psum, h // 2 + 1)
                nc.scalar.activation(lo[:, 0, h * LDV:(h + 1) * LDV],
                                     ps[:, 2 + h // 2, (h % 2) * LDV:(h % 2 + 1) * LDV], ACT.Square,
                                     accum_out=lstat[:, 0, h:h + 1]).then_inc(sq_ready, 1)
            for half in range(2):
                act.wait_ge(loT_psum, half + 1)
                copy(loT[:, 2 * half:2 * half + 2], ps[:, 6 + half, 0:2 * P].rearrange("p (c t) -> p c t", t=P), loT_ready)

            act.wait_ge(xnT_psum, 3)
            copy(xnT[:], ps[:, 0, 0:DC * P].rearrange("p (c t) -> p c t", c=DC), xnT_ready)
            act.wait_ge(below_ready, 1)
            nc.scalar.activation(top_exp[:], below[:], ACT.Exp, accum_out=gate_sum[:, 0:1]).then_inc(top_exp_ready, 1)
            act.wait_ge(xd_psum, 1)
            copy(xd[:, :, 0:P], ps[:, 6, 0:DC * P].rearrange("p (c n) -> p c n", c=DC), xd_ready)
            for n in range(E // 2):
                for half in range(2):
                    act.wait_ge(f1_psum, 2 * n + half + 1)
                    if n >= 1:
                        act.wait_ge(hidT_psum, 2 * (n - 1) + half + 1)
                    copy(hid[:, half * 512:(half + 1) * 512], ps[:, half], hid_ready)
                    if n == 0 and half == 1:
                        act.wait_ge(xd_psum, 3)
                        copy(xd[:, 1, P:], ps[:, 5, 0:E * SLOTS - P], xd_ready)
                for half in range(2):
                    act.wait_ge(hu_ready, 2 * n + half + 1)
                    if n >= 1:
                        act.wait_ge(hT_ready, 2 * (n - 1) + half + 1)
                    nc.scalar.activation(ht[:, 4 * half:4 * half + 4], hu[:, 4 * half:4 * half + 4], ACT.Tanh,
                                         scale=0.5).then_inc(ht_ready, 1)
                if n == 0:
                    act.wait_ge(gatedT_psum, 1)
                    copy(gatedT[:], ps[:, 3].rearrange("p (n t) -> p n t", t=P), gatedT_ready)

        @block.vector
        def _(dve):
            V = nc.vector
            seq = [0]

            def link(ins):
                seq[0] += 1
                ins.then_inc(dve_seq, 1)
                dve.wait_ge(dve_seq, seq[0])

            def norm_stats(n, src):
                link(V.bn_stats(stat[:, n, 0:6], src))
                link(V.bn_aggr(stat[:, n, 6:8], stat[:, n, 0:6]))
                V.tensor_scalar(stat[:, n, 8:9], stat[:, n, 7:8], LN_EPS, None, ALU.add).then_inc(var_ready, 1)

            def normalise(n, dst, src):
                dve.wait_ge(rstd_ready, n + 1)
                return V.tensor_scalar(dst, src, stat[:, n, 6:7], stat[:, n, 9:10], ALU.subtract, ALU.mult)

            def low_part(dst, full, high):
                return V.tensor_tensor(dst, full, high.bitcast(F32), ALU.subtract)

            def split_wk(i):
                dve.wait_ge(wk_high, i + 1)
                low_part(w_k_piece(w_k_l, i), w_k_piece(w_k_stage, i), w_k_piece(w_k_h, i)).then_inc(wk_ready, 1)

            def split_ctxT(n):
                r = n % 2
                if n == 0:
                    dve.wait_ge(ctxT_high, 1)
                else:
                    dve.wait_ge(ld_ctxT[n], 16)
                    if n >= 2:
                        dve.wait_ge(k_psum, G * KT * (n - 1))
                    link(V.tensor_copy(ctxT_h[:, r], stage_t[:, r]))
                low_part(ctxT_l[:, r], stage_t[:, r], ctxT_h[:, r]).then_inc(ctxT_ready, 1)

            def split_ctx(n):
                r = n % 2
                dve.wait_ge(ld_ctx[n], 16)
                if n >= 2:
                    dve.wait_ge(mix_done, G * KT * (n - 1))
                link(V.tensor_copy(ctx_h[:, r], stage_n[:, r]))
                low_part(ctx_l[:, r], stage_n[:, r], ctx_h[:, r]).then_inc(ctx_ready, 1)

            def evacuate(u):
                b, c, g = units[u]
                dve.wait_ge(mix_done, KT * (u + 1))
                for half in range(DC):
                    V.tensor_copy(mixT[:, half, HG * g:HG * (g + 1), b, :],
                                  ps[:, mix_bank(half, g)].rearrange("p (h q) -> p h q", q=S)).then_inc(mixT_ready, 1)

            def add_to_sum(s):
                b, c, g = units[s // KT]
                total = ex_sum[:, HG * g:HG * (g + 1), b, :]
                if s == 0:
                    dve.wait_ge(null_sums, 2)
                else:
                    dve.wait_ge(esum_ready, s)
                V.tensor_tensor(total, total, ex[:, s % NE].rearrange("p (h q) -> p h q", q=S),
                                ALU.add).then_inc(esum_ready, 1)

            V.memset(q_blk[:], 0.0).then_inc(q_blk_zero, 1)
            dve.wait_ge(ld_x, 16)
            norm_stats(0, x0[:])
            normalise(0, xn[:], x0[:]).then_inc(xn_ready, 1)
            split_wk(0)
            split_ctxT(0)
            dve.wait_ge(xnT_psum, 1)
            V.tensor_copy(xnT[:], ps[:, 0, 0:DC * P].rearrange("p (c t) -> p c t", c=DC)).then_inc(xnT_ready, 1)
            split_wk(1)
            dve.wait_ge(q_blk_zero, 1)
            for j in range(2):
                for r in range(2):
                    rows, cols = slice(64 * r, 64 * r + 64), slice(S * r, S * r + S)
                    dve.wait_ge(q_tanh, j + 1)
                    V.tensor_copy(q_blk[rows, 4 * j:4 * j + 4, :, cols],
                                  qT[rows, 4 * j:4 * j + 4].rearrange("p j (b q) -> p j b q", b=B)).then_inc(q_ready, 1)
                split_wk(2 + j)
            split_ctx(0)
            split_ctxT(1)

            for s in range(STEPS):
                u, t = divmod(s, KT)
                b, c, g = units[u]
                r = s % NE
                dve.wait_ge(e_ready, s + 1)
                if s >= NE:
                    dve.wait_ge(mix_done, s - NE + 1)
                low_part(ex_l[:, r], ex[:, r], ex_h[:, r]).then_inc(el_ready, 1)
                if s == 1:
                    add_to_sum(0)
                if s >= 1:
                    add_to_sum(s)
                n = b * NC + c
                if t == 0 and g == G - 1 and n + 1 < B * NC:
                    split_ctx(n + 1)
                if t == KT - 1 and g == G - 1 and n + 2 < B * NC:
                    split_ctxT(n + 2)
                if t == 0 and u >= 2 and units[u - 2][1] == NC - 1:
                    evacuate(u - 2)

            dve.wait_ge(ld_small, 16 * (5 + E))
            V.tensor_tensor(x0[:], x0[:], bout[:], ALU.add).then_inc(x0_ready, 1)
            for g in range(G):
                dve.wait_ge(den_psum, g + 1)
                V.reciprocal(share[:, g], ps[:, den_bank(g)].rearrange("p (j t) -> p j t", t=P)).then_inc(share_ready, 1)
            dve.wait_ge(null_values, 1)
            for g in range(G):
                mine = mixedT[:, PG * g:PG * (g + 1)]
                dve.wait_ge(o_psum, g + 1)
                link(V.tensor_tensor(mine, ps[:, value_bank(g)].rearrange("p (j t) -> p j t", t=P),
                                     null_ex[:, PG * g:PG * (g + 1)], ALU.add))
                dve.wait_ge(share_ready, g + 1)
                V.tensor_tensor(mine, mine, share[:, g], ALU.mult).then_inc(o_ready, 1)

            dve.wait_ge(wo_psum, 1)
            norm_stats(1, ps[:, 2, 0:D])
            normalise(1, xn[:], ps[:, 2, 0:D]).then_inc(xn_ready, 1)
            V.tensor_copy(x1[:], ps[:, 2, 0:D]).then_inc(x1_ready, 1)
            dve.wait_ge(low_psum, 1)
            dve.wait_ge(zero_ready, 3)
            V.tensor_copy(lowT[0:LR], ps[0:LR, 3, 0:P]).then_inc(low_ready, 1)
            dve.wait_ge(qk_psum, 1)
            qk = ps[:, 1].rearrange("p (w j t) -> p w j t", w=2, j=2)

            def scaled_queries(r):
                rows = slice(64 * r, 64 * r + 64)
                V.tensor_scalar(lqT[rows, :, r, :], qk[rows, 0], LDK ** -0.5, None, ALU.mult).then_inc(qk_ready, 1)

            scaled_queries(0)
            dve.wait_ge(gln_ready, 1)
            V.scalar_tensor_tensor(out=gate[:, 3], in0=ps[:, 3, D:2 * D], scalar=0.0, in1=gate[:, 2], op0=ALU.min,
                                   op1=ALU.subtract).then_inc(g_ready, 1)
            scaled_queries(1)
            V.tensor_copy(lkT[:], qk[:, 1]).then_inc(qk_ready, 1)
            dve.wait_ge(qk_ready, 3)

            def decayed_queries(pair, levels):
                for n in levels:
                    half = LEVELS[n]
                    right = lqT[:, pair].rearrange("p r (m w l) -> p r m w l", w=2, l=half)[:, :, :, 1, :]
                    dec = decay[:, pair, n].rearrange("p (m w l) -> p m w l", w=2, l=half)[:, :, 1, :]
                    dec = dec.unsqueeze(1).broadcast_to([P, 2, 64 // half, half])
                    V.tensor_tensor(qx[:, pair, n].rearrange("p r (m l) -> p r m l", l=half), right, dec,
                                    ALU.mult).then_inc(qx_ready, 1)

            dve.wait_ge(dec_ready, 1)
            V.tensor_tensor(kx[:, 0, 0:4], decay[:, 0, 0:4], lkT[:, 0].unsqueeze(1).broadcast_to([P, 4, P]),
                            ALU.mult).then_inc(kx_ready, 1)
            decayed_queries(0, range(4))
            dve.wait_ge(dec_ready, 2)
            decayed_queries(1, range(4))
            dve.wait_ge(dec_ready, 3)
            for pair in range(2):
                decayed_queries(pair, range(4, NL))
            dve.wait_ge(own_psum, 1)
            for pair in range(2):
                V.tensor_tensor(att[:, 2 * pair:2 * pair + 2], ps[:, 0, 256 * pair:256 * pair + 256].rearrange("p (h t) -> p h t", t=P),
                                eye.unsqueeze(1).broadcast_to([P, 2, P]), ALU.mult).then_inc(att_ready, 1)
            for n, half in enumerate(LEVELS):
                dve.wait_ge(lev_psum, 1 + n // 2)
                for pair in range(2):
                    at = 256 * (n % 2) + 128 * pair
                    src = ps[:, (1, 6, 7)[n // 2], at:at + 128].rearrange("p (h m l) -> p h m l", h=2, l=half)
                    mask = const[:, C_MASK + 64 * n:C_MASK + 64 * n + 64].bitcast(U32).rearrange("p (m l) -> p m l", l=half)
                    mask = mask.unsqueeze(1).broadcast_to([P, 2, 64 // half, half])
                    dst = att[:, 2 * pair:2 * pair + 2].rearrange("p h (m w l) -> p h m w l", w=2, l=half)[:, :, :, 1, :]
                    dve.wait_ge(att_ready, 2 * n + pair + 1)
                    V.copy_predicated(dst, mask, src).then_inc(att_ready, 1)
            dve.wait_ge(gtanh_ready, 1)
            link(V.scalar_tensor_tensor(out=silu[:, 1], in0=silu[:, 0], scalar=1.0, in1=ps[:, 5], op0=ALU.add,
                                        op1=ALU.mult))
            V.tensor_tensor(lo[:, 1].rearrange("p (h d) -> p h d", d=LDV),
                            silu[:, 1].rearrange("p (h d) -> p h d", d=LDV),
                            gnorm[:].unsqueeze(1).broadcast_to([P, LH, LDV]), ALU.mult).then_inc(gain_ready, 1)
            dve.wait_ge(sq_ready, 4)
            V.tensor_scalar(lstat[:, 1], lstat[:, 0], 4.0 / LDV, 4.0 * LN_EPS, ALU.mult, ALU.add).then_inc(ms_ready, 1)
            dve.wait_ge(lr_ready, 1)
            dve.wait_ge(gain_ready, 1)
            for h in range(LH):
                V.scalar_tensor_tensor(out=lo[:, 2, h * LDV:(h + 1) * LDV],
                                       in0=ps[:, 2 + h // 2, (h % 2) * LDV:(h % 2 + 1) * LDV],
                                       scalar=lstat[:, 2, h:h + 1], in1=lo[:, 1, h * LDV:(h + 1) * LDV],
                                       op0=ALU.mult, op1=ALU.mult).then_inc(lo_ready, 1)

            dve.wait_ge(lw_psum, 1)
            norm_stats(2, ps[:, 4, 0:D])
            normalise(2, xn[:], ps[:, 4, 0:D]).then_inc(xn_ready, 1)
            V.tensor_tensor(x2[:], ps[:, 4, 0:D], beta[:], ALU.add).then_inc(x2_ready, 1)
            dve.wait_ge(xn_ready, 3)
            link(V.tensor_copy(xn_h[:], xn[:]))
            low_part(xn_l[:], xn[:], xn_h[:]).then_inc(xn_split, 1)
            dve.wait_ge(rl_psum, 1)
            logits = ps[:, 1, 0:E]
            link(V.max(top[:], logits))
            link(V.max_index(top_idx[:], top[:], logits))
            V.tensor_tensor(pick[:], iota8.unsqueeze(1).broadcast_to([P, 2, E]),
                            top_idx[:, 0:2].unsqueeze(2).broadcast_to([P, 2, E]), ALU.is_equal).then_inc(pick_ready, 1)
            V.tensor_scalar(below[:], top[:], top[:, 0:1], None, ALU.subtract).then_inc(below_ready, 1)
            dve.wait_ge(loc_psum, 1)
            places = ps[:, 2, 0:2 * E].rearrange("p (k e) -> p k e", k=2)
            V.tensor_tensor(place[:], places, first_slot.unsqueeze(1).broadcast_to([P, 2, E]),
                            ALU.add)
            link(V.scalar_tensor_tensor(out=kept[:], in0=places, scalar=float(CAP), in1=pick[:], op0=ALU.is_lt,
                                        op1=ALU.mult))
            for k in range(2):
                ins = V.scalar_tensor_tensor(out=picked[:, k], in0=kept[:, k], scalar=1.0, in1=place[:, k],
                                             op0=ALU.mult, op1=ALU.mult, accum_out=slot[:, k:k + 1])
            link(ins)

            def one_hot(cols):
                link(V.tensor_scalar(onehot[:, cols], slot_no[:, cols], slot[:, 0:1], None, ALU.is_equal))
                V.scalar_tensor_tensor(out=onehot[:, cols], in0=slot_no[:, cols], scalar=slot[:, 1:2],
                                       in1=onehot[:, cols].bitcast(F32), op0=ALU.is_equal, op1=ALU.add).then_inc(oh_ready, 1)

            one_hot(slice(0, P))
            one_hot(slice(P, E * SLOTS))
            dve.wait_ge(top_exp_ready, 1)
            link(V.tensor_reduce(gate_sum[:, 1:2], top_exp[:, 0:2], AX.X, ALU.add))
            link(V.scalar_tensor_tensor(out=gate_sum[:, 2:3], in0=gate_sum[:, 0:1], scalar=GATE_EPS,
                                        in1=gate_sum[:, 1:2], op0=ALU.mult, op1=ALU.max))
            link(V.reciprocal(gate_sum[:, 3:4], gate_sum[:, 2:3]))
            link(V.tensor_scalar(gates[:], top_exp[:, 0:2], gate_sum[:, 3:4], None, ALU.mult))
            dve.wait_ge(xd_psum, 2)
            V.tensor_copy(xd[:, 0, P:], ps[:, 3, 0:E * SLOTS - P]).then_inc(xd_ready, 1)

            def gated_one_hot():
                for k in range(2):
                    ins = V.tensor_scalar(gated[:, k], slot_no, slot[:, k:k + 1], gates[:, k:k + 1], ALU.is_equal,
                                          ALU.mult)
                link(ins)
                V.tensor_tensor(gated[:, 0], gated[:, 0], gated[:, 1], ALU.add).then_inc(gated_ready, 1)

            dve.wait_ge(zero_ready, 4)

            def bias_and_silu(n):
                for half in range(2):
                    chunks = slice(4 * half, 4 * half + 4)
                    dve.wait_ge(hidT_psum, 2 * n + half + 1)
                    if n >= 1:
                        dve.wait_ge(hT_ready, 2 * (n - 1) + half + 1)
                    bias = b1[:, 2 * n:2 * n + 2, chunks].rearrange("p e c -> p c e").unsqueeze(3)
                    V.tensor_tensor(hu[:, chunks],
                                    ps[:, 6 + half].rearrange("p (c e s) -> p c e s", c=4, e=2)[:, :, :, 0:CAP],
                                    bias.broadcast_to([P, 4, 2, CAP]), ALU.add).then_inc(hu_ready, 1)
                for half in range(2):
                    chunks = slice(4 * half, 4 * half + 4)
                    dve.wait_ge(ht_ready, 2 * n + half + 1)
                    if n >= 2:
                        dve.wait_ge(y_psum, n - 1)
                    V.scalar_tensor_tensor(out=hT[:, n % 2, chunks, :, 0:CAP], in0=ht[:, chunks], scalar=1.0,
                                           in1=hu[:, chunks], op0=ALU.add, op1=ALU.mult).then_inc(hT_ready, 1)

            def rows_out(n):
                dve.wait_ge(y_psum, n + 1)
                if n >= 2:
                    dve.wait_ge(c_psum, n - 1)
                V.scalar_tensor_tensor(out=ysb[:, n % 2], in0=ps[:, Y_BANK[n % 2], 0:D], scalar=0.5, in1=b2[:, n],
                                       op0=ALU.mult, op1=ALU.add).then_inc(y_ready, 1)

            bias_and_silu(0)
            gated_one_hot()
            rows_out(0)
            bias_and_silu(1)
            rows_out(1)
            bias_and_silu(2)
            bias_and_silu(3)
            rows_out(2)
            rows_out(3)
            dve.wait_ge(c_psum, E // 2)
            norm_stats(3, ps[:, 4, 0:D])
            link(V.scalar_tensor_tensor(out=fin[:, 0], in0=ps[:, 4, 0:D], scalar=stat[:, 3, 6:7], in1=gamma[:],
                                        op0=ALU.subtract, op1=ALU.mult))
            dve.wait_ge(rstd_ready, 4)
            dve.wait_ge(x2_ready, 1)
            V.scalar_tensor_tensor(out=fin[:, 1], in0=fin[:, 0], scalar=stat[:, 3, 9:10], in1=x2[:],
                                   op0=ALU.mult, op1=ALU.add).then_inc(out_ready, 1)

        @block.tensor
        def _(pe):
            MM = nc.tensor.matmul

            def warm(n, bank):
                for _ in range(n):
                    MM(ps[:, bank], warmer[:, 0:P], warmer[:], start=True, stop=True)

            def transpose_xn(n):
                pe.wait_ge(xn_ready, n + 1)
                for c in range(DC):
                    last = nc.tensor.transpose(ps[:, 0, c * P:(c + 1) * P], xn[:, c * P:(c + 1) * P], eye)
                last.then_inc(xnT_psum, 1)

            def split_product(dst, lhs, rhs, start, stop):
                parts = [(0, 0), (0, 1), (1, 0)]
                for m, (i, j) in enumerate(parts):
                    last = MM(dst, lhs[i], rhs[j], start=start and m == 0, stop=stop and m == len(parts) - 1)
                return last

            def project_keys(kp):
                u, i = divmod(kp, KT)
                b, c, g = units[u]
                n = b * NC + c
                pe.wait_ge(ctxT_ready, n + 1)
                pe.wait_ge(wk_ready, KT * g + i + 1)
                if kp >= 2:
                    pe.wait_ge(k_ready, kp - 1)
                for j in range(PK):
                    cols = slice((PK * i + j) * P, (PK * i + j + 1) * P)
                    for d in range(DC):
                        last = split_product(ps[:, K_BANK + kp % 2, j * CK:(j + 1) * CK],
                                             [w[:, g, d, cols] for w in (w_k_h, w_k_l)],
                                             [x[:, n % 2, d, :] for x in (ctxT_h, ctxT_l)], d == 0, d == DC - 1)
                last.then_inc(k_psum, 1)

            def scores(s):
                u, t = divmod(s, KT)
                b, c, g = units[u]
                pe.wait_ge(k_ready, KT * (u + 1))
                if s >= 2:
                    pe.wait_ge(e_ready, s - 1)
                for j in range(PG):
                    last = MM(ps[:, S_BANK + s % 2, j * P:(j + 1) * P], keys[:, u % 2, j, t * P:(t + 1) * P],
                              q_blk[:, g * PG + j, b, :], start=True, stop=True)
                last.then_inc(s_psum, 1)

            def weighted_sum(s):
                u, t = divmod(s, KT)
                b, c, g = units[u]
                n = b * NC + c
                pe.wait_ge(el_ready, s + 1)
                pe.wait_ge(ctx_ready, n + 1)
                if b == 1 and c == 0 and t == 0:
                    pe.wait_ge(mixT_ready, DC * (g + 1))
                for half in range(DC):
                    cols = slice(half * P, (half + 1) * P)
                    last = split_product(ps[:, mix_bank(half, g)], [x[:, n % 2, t, cols] for x in (ctx_h, ctx_l)],
                                         [x[:, s % NE, :] for x in (ex_h, ex_l)], c == 0 and t == 0,
                                         c == NC - 1 and t == KT - 1)
                last.then_inc(mix_done, 1)

            def denominators(g):
                pe.wait_ge(esum_ready, STEPS - (G - 1 - g) * KT)
                for j in range(PG):
                    for r in range(2):
                        h = HG * g + 2 * j + r
                        last = MM(ps[64 * r:64 * r + 64, den_bank(g), j * P:(j + 1) * P], ones[:, 0:DH],
                                  ex_sum[:, h].rearrange("p b q -> p (b q)"), start=True, stop=True)
                last.then_inc(den_psum, 1)

            def values(g):
                pe.wait_ge(mixT_ready, G * DC)
                pe.wait_ge(mixT_last, DC * (g + 1))
                pe.wait_ge(ld_wv, 32)
                for j in range(PG):
                    for half in range(DC):
                        for r in range(2):
                            h = HG * g + 2 * j + r
                            last = MM(ps[64 * r:64 * r + 64, value_bank(g), j * P:(j + 1) * P],
                                      w_v[:, half, h * DH:(h + 1) * DH],
                                      mixT[:, half, h].rearrange("p b q -> p (b q)"), start=half == 0,
                                      stop=half == DC - 1)
                last.then_inc(o_psum, 1)

            def output(g):
                if g == 0:
                    pe.wait_ge(x0_ready, 1)
                    pe.wait_ge(mixT_last, DC)
                    MM(ps[:, 2, 0:D], eye, x0[:], start=True, stop=False)
                pe.wait_ge(o_ready, g + 1)
                for n in range(4 * g, 4 * g + 4):
                    last = MM(ps[:, 2, 0:D], mixedT[:, n], w_out[:, n], start=False, stop=n == FC - 1)
                if g == G - 1:
                    last.then_inc(wo_psum, 1)

            pe.wait_ge(warmer_ready, 1)
            warm(8, 7)
            pe.wait_ge(ld_eye, 16)
            transpose_xn(0)
            warm(2, 7)
            project_keys(0)
            pe.wait_ge(xnT_ready, 1)
            for j in range(NPAIR):
                if j % 4 == 0:
                    pe.wait_ge(ld_wq[j // 4], 16)
                for c in range(DC):
                    last = MM(ps[:, 1 + j // 4, (j % 4) * P:(j % 4 + 1) * P], w_q[:, c, j * P:(j + 1) * P],
                              xnT[:, c], start=c == 0, stop=c == DC - 1)
                if j % 4 == 3:
                    last.then_inc(q_psum, 1)
            project_keys(1)
            pe.wait_ge(q_tanh, 2)
            pe.wait_ge(nk_tanh, 1)
            for j in range(2):
                MM(ps[:, NULL_BANK[j]], null_kt[:], qT[:, 4 * j:4 * j + 4].rearrange("p j t -> p (j t)"), start=True,
                   stop=True).then_inc(null_psum, 1)
            project_keys(2)
            pe.wait_ge(q_ready, 4)
            LAG = 2
            for s in range(STEPS):
                if s == LAG:
                    pe.wait_ge(null_ready, 2)
                scores(s)
                if s + AHEAD < STEPS:
                    project_keys(s + AHEAD)
                if s == STEPS - 1:
                    pe.wait_ge(k_ready, STEPS)
                    denominators(0)
                if s >= LAG:
                    weighted_sum(s - LAG)
            weighted_sum(STEPS - 2)
            pe.wait_ge(e_ready, STEPS)
            denominators(1)
            weighted_sum(STEPS - 1)
            values(0)
            values(1)
            output(0)
            output(1)

            warm(4, 7)
            transpose_xn(1)
            pe.wait_ge(xnT_ready, 2)
            pe.wait_ge(ld_lin, 16 * 8)
            pe.wait_ge(ld_const, 16)
            for c in range(DC):
                last = MM(ps[0:LR, 3, 0:P], w_gk1[:, c], xnT[:, c], start=c == 0, stop=c == DC - 1)
            last.then_inc(low_psum, 1)

            def queries_or_keys(w, weight):
                for j in range(2):
                    for c in range(DC):
                        last = MM(ps[:, 1, (2 * w + j) * P:(2 * w + j + 1) * P], weight[:, c, j * P:(j + 1) * P],
                                  xnT[:, c], start=c == 0, stop=c == DC - 1)
                return last

            queries_or_keys(0, w_lq)
            pe.wait_ge(low_ready, 1)
            MM(ps[:, 3, D:2 * D], lowT[0:LR + 1], w_gk2[0:LR + 1], start=True, stop=True).then_inc(logit_psum, 1)
            queries_or_keys(1, w_lk).then_inc(qk_psum, 1)
            MM(ps[:, 4], xnT[:, 0], w_lv[:, 0], start=True, stop=False)
            MM(ps[:, 5], xnT[:, 0], w_lg[:, 0], start=True, stop=False)
            pe.wait_ge(g_ready, 1)
            for pair in range(2):
                MM(ps[:, 6 + pair], gate[:, 3, pair * P:(pair + 1) * P], const[:, C_DECAY:C_DECAY + 4 * P], start=True,
                   stop=True).then_inc(dec_psum, 1)
            for pair in range(2):
                last = MM(ps[:, 2, 2 * pair * P:2 * (pair + 1) * P], gate[:, 3, pair * P:(pair + 1) * P],
                          const[:, C_DECAY + 4 * P:C_DECAY + NL * P], start=True, stop=True)
            last.then_inc(dec_psum, 1)
            pe.wait_ge(qk_ready, 3)
            for pair in range(2):
                last = MM(ps[:, 0, 2 * pair * P:2 * (pair + 1) * P], lkT[:, pair], lqT[:, pair], start=True, stop=True)
            last.then_inc(own_psum, 1)
            MM(ps[:, 4], xnT[:, 1], w_lv[:, 1], start=False, stop=True).then_inc(v_psum, 1)
            pe.wait_ge(dec_ready, 2)
            for n in range(NL):
                for pair in range(2):
                    if n < 4:
                        if pair == 0:
                            pe.wait_ge(kx_ready, 1)
                        else:
                            pe.wait_ge(kx_pool, 1)
                        pe.wait_ge(qx_ready, 4 * pair + n + 1)
                    else:
                        pe.wait_ge(kx_pool, 2 + pair)
                        pe.wait_ge(qx_ready, 8 + 2 * pair + n - 4 + 1)
                    at = 256 * (n % 2) + 128 * pair
                    last = MM(ps[:, (1, 6, 7)[n // 2], at:at + 128], kx[:, pair, n], qx[:, pair, n], start=True,
                              stop=True)
                if n % 2:
                    last.then_inc(lev_psum, 1)
            MM(ps[:, 5], xnT[:, 1], w_lg[:, 1], start=False, stop=True).then_inc(g_psum, 1)
            pe.wait_ge(v_ready, 1)
            for h in range(LH):
                pe.wait_ge(att_ready, 2 * NL + 1 + h // 2)
                last = MM(ps[:, 2 + h // 2, (h % 2) * LDV:(h % 2 + 1) * LDV], att[:, h], lv[:, h * LDV:(h + 1) * LDV],
                          start=True, stop=True)
                if h % 2:
                    last.then_inc(lo_psum, 1)
            pe.wait_ge(x1_ready, 1)
            MM(ps[:, 4, 0:D], eye, x1[:], start=True, stop=False)
            warm(6, 0)
            for h in range(LH):
                pe.wait_ge(lo_ready, h + 1)
                last = nc.tensor.transpose(ps[:, 6 + h // 2, (h % 2) * P:(h % 2 + 1) * P], lo[:, 2, h * P:(h + 1) * P], eye)
                if h % 2:
                    last.then_inc(loT_psum, 1)
            for h in range(LH):
                pe.wait_ge(loT_ready, h // 2 + 1)
                last = MM(ps[:, 4, 0:D], loT[:, h], w_lo[:, h], start=False, stop=h == LH - 1)
            last.then_inc(lw_psum, 1)

            warm(6, 7)
            transpose_xn(2)
            warm(2, 7)
            pe.wait_ge(xnT_ready, 3)
            for c in range(DC):
                last = MM(ps[:, 1, 0:E], xnT[:, c], w_route[:, c], start=c == 0, stop=c == DC - 1)
            last.then_inc(rl_psum, 1)
            pe.wait_ge(x2_ready, 1)
            MM(ps[:, 4, 0:D], eye, xn[:], start=True, stop=False)
            warm(1, 7)
            pe.wait_ge(triangle_ready, 2)
            pe.wait_ge(pick_ready, 1)
            MM(ps[:, 2, 0:2 * E], strict_b[:], pick[:].rearrange("p k e -> p (k e)"), start=True, stop=False,
               skip_group_check=True)
            MM(ps[:, 2, E:2 * E], ones_b[:], pick[:, 0], start=False, stop=True, skip_group_check=True).then_inc(loc_psum, 1)
            warm(6, 7)

            def dispatch(dst, c, cols):
                MM(dst, xn_h[:, c * P:(c + 1) * P], onehot[:, cols], start=True, stop=False)
                return MM(dst, xn_l[:, c * P:(c + 1) * P], onehot[:, cols], start=False, stop=True)

            pe.wait_ge(xn_split, 1)
            pe.wait_ge(oh_ready, 1)
            for c in range(DC):
                last = dispatch(ps[:, 6, c * P:(c + 1) * P], c, slice(0, P))
            last.then_inc(xd_psum, 1)
            warm(2, 7)
            pe.wait_ge(xd_ready, 1)

            def up(n):
                for j in range(2):
                    pe.wait_ge(ld_exp[2 * n + j], 32)
                for half in range(2):
                    if n:
                        pe.wait_ge(hid_ready, 2 * (n - 1) + half + 1)
                    for c in range(DC):
                        for j in range(2):
                            e = 2 * n + j
                            last = MM(ps[SLOTS * j:SLOTS * (j + 1), half], xd[:, c, e * SLOTS:(e + 1) * SLOTS],
                                      w1[e][:, c, half * 512:(half + 1) * 512], start=c == 0, stop=c == DC - 1)
                    last.then_inc(f1_psum, 1)

            def turn(n):
                for half in range(2):
                    pe.wait_ge(hid_ready, 2 * n + half + 1)
                    if n:
                        pe.wait_ge(hu_ready, 2 * (n - 1) + half + 1)
                    for c in range(4):
                        last = nc.tensor.transpose(ps[:, 6 + half, c * P:(c + 1) * P],
                                                   hid[:, (4 * half + c) * P:(4 * half + c + 1) * P], eye)
                    last.then_inc(hidT_psum, 1)

            def down(n):
                pe.wait_ge(hT_ready, 2 * n + 2)
                if n >= 2:
                    pe.wait_ge(y_ready, n - 1)
                for c in range(FC):
                    for j in range(2):
                        last = MM(ps[SLOTS * j:SLOTS * (j + 1), Y_BANK[n % 2], 0:D], hT[:, n % 2, c, j], w2[2 * n + j][:, c],
                                  start=c == 0, stop=c == FC - 1)
                last.then_inc(y_psum, 1)

            def combine(n):
                pe.wait_ge(y_ready, n + 1)
                if n == 0:
                    pe.wait_ge(gatedT_ready, 1)
                MM(ps[:, 4, 0:D], gatedT[:, n], ysb[:, n % 2], start=False, stop=n == E // 2 - 1).then_inc(c_psum, 1)

            up(0)
            pe.wait_ge(oh_ready, 2)
            for c in range(DC):
                dispatch(ps[:, (3, 5)[c], 0:E * SLOTS - P], c, slice(P, E * SLOTS)).then_inc(xd_psum, 1)
            turn(0)
            pe.wait_ge(xd_ready, 3)
            up(1)
            pe.wait_ge(gated_ready, 1)
            for n in range(E // 2):
                last = nc.tensor.transpose(ps[:, 3, n * P:(n + 1) * P], gated[:, 0, n * P:(n + 1) * P], eye)
            last.then_inc(gatedT_psum, 1)
            down(0)
            turn(1)
            up(2)
            combine(0)
            down(1)
            turn(2)
            up(3)
            combine(1)
            turn(3)
            down(2)
            down(3)
            combine(2)
            combine(3)


_PLAIN = {
    "Wq": "L0_xattn_Wq", "Wkv": "L0_xattn_Wkv", "Wout": "L0_xattn_Wout", "bout": "L0_xattn_bout",
    "lWq": "L0_attn_Wq", "lWk": "L0_attn_Wk", "lWv": "L0_attn_Wv", "lWg": "L0_attn_Wg", "lWo": "L0_attn_Wo",
    "Wgk1": "L0_attn_Wgk1", "gnorm": "L0_attn_g_norm_weight", "wg": "L0_ffn_wg", "fc2": "L0_ffn_fc2_w",
    "b2": "L0_ffn_fc2_b", "gamma": "L0_ffn_ln_gamma", "beta": "L0_ffn_ln_beta",
}


def kernel(**inputs):
    import concourse.bacc as _bacc
    from concourse.bass_utils import run_bass_kernel_spmd as _run

    v = {k: np.ascontiguousarray(x) for k, x in inputs.items()}
    arrays = {short: v[name] for short, name in _PLAIN.items()}
    arrays["x"] = v["x"].reshape(P, D)
    arrays["ctx"] = v["ctx_1024"].reshape(B * NK, D)
    arrays["ctxT"] = arrays["ctx"].T
    arrays["Wgk2b"] = np.concatenate([v["L0_attn_Wgk2"], v["L0_attn_bgk2"][None, :]])
    arrays["fc1T"] = v["L0_ffn_fc1_w"].transpose(0, 2, 1)
    arrays["b1"] = v["L0_ffn_fc1_b"].reshape(E, FC, P).transpose(2, 0, 1)
    null_k = np.zeros((P, P), np.float32)
    for r in range(2):
        null_k[DH * r:DH * (r + 1), DH * r:DH * (r + 1)] = v["L0_xattn_null_key"][:, None]
    arrays["null_k"], arrays["null_v"] = null_k, np.tile(v["L0_xattn_null_value"], 2)[:, None]
    arrays["const"] = shape_constants()

    nc = _bacc.Bacc("TRN2", target_bir_lowering=False, num_devices=1)
    feed, a = {}, {}
    for name, x in arrays.items():
        feed[f"in_{name}"] = x = np.ascontiguousarray(x)
        a[name] = nc.dram_tensor(f"in_{name}", x.shape, mybir.dt.from_np(x.dtype), kind="ExternalInput").ap()
    out = nc.dram_tensor("out_x", (P, D), F32, kind="ExternalOutput").ap()
    block_kernel(nc, a, out)
    r = _run(nc, [feed], core_ids=[0])
    return r.results[0]["out_x"].reshape(B, S, D)
```
